# Optimizing a Trainium2 kernel written in Bass

```python
import numpy as np
import jax
import jax.numpy as jnp

def _softmax(x, axis=-1):
    return jax.nn.softmax(x, axis=axis)

def _gelu(x):
    return jax.nn.gelu(x, approximate=True)

def _silu(x):
    return jax.nn.silu(x)

def _sigmoid(x):
    return jax.nn.sigmoid(x)

def _layernorm(x, axis=-1, eps=1e-05):
    m = jnp.mean(x, axis=axis, keepdims=True)
    v = jnp.var(x, axis=axis, keepdims=True)
    return (x - m) / jnp.sqrt(v + eps)

def _scatter_add(tgt, idx, src, axis=0):
    return tgt.at[idx].add(src)

def _segment_sum(src, seg, n):
    return jax.ops.segment_sum(src, seg, n)
kernel_name = 'mk_seq_preln_d1_jaxref_r4_292138'

def setup_inputs(seed: int=0):
    np.random.seed(seed)
    _w = jnp.asarray

    def _L0_attn_setup():
        import jax, jax.numpy as jnp
        import numpy as np
        DIM = 256
        N_HEADS = 16
        HEAD_DIM = DIM // N_HEADS
        D_LATENT = 64
        B, T = (1, 1024)
        key = jax.random.key(seed)
        ks = jax.random.split(key, 6)
        s = 0.02
        return {'x': jax.random.normal(ks[0], (B, T, DIM), dtype=jnp.float32), 'W_DKV': jax.random.normal(ks[1], (DIM, D_LATENT), dtype=jnp.float32) * s, 'W_UK': jax.random.normal(ks[2], (D_LATENT, DIM), dtype=jnp.float32) * s, 'W_UV': jax.random.normal(ks[3], (D_LATENT, DIM), dtype=jnp.float32) * s, 'W_UQ': jax.random.normal(ks[4], (DIM, DIM), dtype=jnp.float32) * s, 'W_O': jax.random.normal(ks[5], (DIM, DIM), dtype=jnp.float32) * s}
    _L0_attn_in = _L0_attn_setup()

    def _L0_ffn_setup():
        import jax, jax.numpy as jnp
        import numpy as np
        D_MODEL = 256
        D_FF = 512
        NUM_EXPERTS = 8
        TOP_K = 2
        BATCH, SEQ = (2, 512)
        key = jax.random.key(seed)
        ks = jax.random.split(key, 5)
        s = 0.02
        x = jax.random.normal(ks[0], (BATCH, SEQ, D_MODEL), jnp.float32)
        Wr = jax.random.normal(ks[1], (D_MODEL, NUM_EXPERTS), jnp.float32) * s
        temp = jnp.ones((1,), jnp.float32)
        W1 = jax.random.normal(ks[2], (NUM_EXPERTS, D_MODEL, 2 * D_FF), jnp.float32) * s
        b1 = jnp.zeros((NUM_EXPERTS, 2 * D_FF), jnp.float32)
        W2 = jax.random.normal(ks[3], (NUM_EXPERTS, D_FF, D_MODEL), jnp.float32) * s
        b2 = jnp.zeros((NUM_EXPERTS, D_MODEL), jnp.float32)
        return {'x': x, 'Wr': Wr, 'temp': temp, 'W1': W1, 'b1': b1, 'W2': W2, 'b2': b2}
    _L0_ffn_in = _L0_ffn_setup()
    _d = {'L0_attn_x': _L0_attn_in['x'], 'L0_attn_W_DKV': _L0_attn_in['W_DKV'], 'L0_attn_W_UK': _L0_attn_in['W_UK'], 'L0_attn_W_UV': _L0_attn_in['W_UV'], 'L0_attn_W_UQ': _L0_attn_in['W_UQ'], 'L0_attn_W_O': _L0_attn_in['W_O'], 'L0_ffn_Wr': _L0_ffn_in['Wr'], 'L0_ffn_temp': _L0_ffn_in['temp'], 'L0_ffn_W1': _L0_ffn_in['W1'], 'L0_ffn_b1': _L0_ffn_in['b1'], 'L0_ffn_W2': _L0_ffn_in['W2'], 'L0_ffn_b2': _L0_ffn_in['b2']}
    _x0 = _d['L0_attn_x']
    _d['L0_attn_x'] = jax.random.normal(jax.random.fold_in(jax.random.key(seed), 1), (4, 1024, 256), dtype=_x0.dtype)
    del _x0
    return _d

def reference(L0_attn_x, L0_attn_W_DKV, L0_attn_W_UK, L0_attn_W_UV, L0_attn_W_UQ, L0_attn_W_O, L0_ffn_Wr, L0_ffn_temp, L0_ffn_W1, L0_ffn_b1, L0_ffn_W2, L0_ffn_b2):

    def _L0_attn_ref(x, W_DKV, W_UK, W_UV, W_UQ, W_O):
        import jax, jax.numpy as jnp
        import numpy as np
        DIM = 256
        N_HEADS = 16
        HEAD_DIM = DIM // N_HEADS
        D_LATENT = 64
        B, T = (1, 1024)
        b, t, d = x.shape
        h, hd = (N_HEADS, HEAD_DIM)
        c_kv = x @ W_DKV
        k = (c_kv @ W_UK).reshape(b, t, h, hd)
        v = (c_kv @ W_UV).reshape(b, t, h, hd)
        q = (x @ W_UQ).reshape(b, t, h, hd)
        scale = 1.0 / jnp.sqrt(jnp.asarray(hd, x.dtype))
        scores = jnp.einsum('bqhd,bkhd->bhqk', q, k) * scale
        causal = jnp.tril(jnp.ones((t, t), dtype=bool))
        scores = jnp.where(causal, scores, jnp.asarray(-jnp.inf, scores.dtype))
        probs = jax.nn.softmax(scores, axis=-1)
        ctx = jnp.einsum('bhqk,bkhd->bqhd', probs, v).reshape(b, t, d)
        return ctx @ W_O

    def _L0_ffn_ref(x, Wr, temp, W1, b1, W2, b2):
        import jax, jax.numpy as jnp
        import numpy as np
        D_MODEL = 256
        D_FF = 512
        NUM_EXPERTS = 8
        TOP_K = 2
        BATCH, SEQ = (2, 512)
        B, S, D = x.shape
        xf = x.reshape(-1, D)
        logits = xf @ Wr / temp
        topw, topi = jax.lax.top_k(logits, TOP_K)
        topw = jax.nn.softmax(topw, axis=-1)
        out = jnp.zeros_like(xf)
        for e in range(NUM_EXPERTS):
            h = xf @ W1[e] + b1[e]
            a, g = jnp.split(h, 2, axis=-1)
            y = a * jax.nn.silu(g) @ W2[e] + b2[e]
            we = jnp.sum(jnp.where(topi == e, topw, 0.0), axis=-1, keepdims=True)
            out = out + y * we
        return out.reshape(B, S, D)
    x = L0_attn_x
    x = x + _L0_attn_ref(_layernorm(x, axis=-1), L0_attn_W_DKV, L0_attn_W_UK, L0_attn_W_UV, L0_attn_W_UQ, L0_attn_W_O)
    x = x + _L0_ffn_ref(_layernorm(x, axis=-1), L0_ffn_Wr, L0_ffn_temp, L0_ffn_W1, L0_ffn_b1, L0_ffn_W2, L0_ffn_b2)
    return x

_drawn_inputs = setup_inputs


def setup_inputs(seed=0):
    import zlib

    import numpy as np

    out = dict(_drawn_inputs(seed))
    spreads = {'L0_ffn_b1': (0.0, 0.8), 'L0_ffn_b2': (0.0, 0.8)}
    factors = {'L0_attn_W_DKV': 8.0,
     'L0_attn_W_UK': 8.0,
     'L0_attn_W_UV': 8.0,
     'L0_attn_W_UQ': 8.0,
     'L0_attn_W_O': 8.0,
     'L0_ffn_W1': 3.029,
     'L0_ffn_W2': 3.007}
    for name, (base, spread) in spreads.items():
        noise = np.random.default_rng([zlib.crc32(name.encode()), seed]).standard_normal(out[name].shape)
        drawn = base * np.exp(spread * noise) if base else spread * noise
        out[name] = jnp.asarray(drawn.astype(out[name].dtype))
    for name, factor in factors.items():
        out[name] = (out[name] * factor).astype(out[name].dtype)
    return out
```

```python
from contextlib import ExitStack

import concourse.bass as bass
from concourse import mybir

F32 = mybir.dt.float32
BF16 = mybir.dt.bfloat16
I32 = mybir.dt.int32
U32 = mybir.dt.uint32
ALU = mybir.AluOpType
ACT = mybir.ActivationFunctionType
AX = mybir.AxisListType

P = 128
BATCH, SEQ, D = 4, 1024, 256
NTOK = BATCH * SEQ
DC = D // P
LAT = 64
HEADS, HD = 16, 16
QUAD = 4
NQUAD = BATCH * HEADS // QUAD
CHUNK = 512
NCHUNK = NTOK // CHUNK
TPC = CHUNK // P
NTILE = NTOK // P
QT = SEQ // P
EPS = 1e-5
LN_STEPS = 7
SCALE = HD ** -0.5
PARTS = 3
Q_PART = [0, 0, 0, 1, 1, 2]
K_PART = [0, 1, 2, 0, 1, 0]
STACK = HD * len(Q_PART)
MAXROWS = STACK + PARTS
MASKED = -3.0e38


def project_phase(nc, dram, x, w_dkv, w_uk, w_uv, w_uq):
    with ExitStack() as ctx:
        def sb(name, shape, dt=F32):
            return ctx.enter_context(nc.sbuf_tensor(name, shape, dt))

        def ps(name, shape, dt=F32):
            return ctx.enter_context(nc.psum_tensor(name, shape, dt))

        def sem(name):
            return ctx.enter_context(nc.semaphore(name))

        def pair(make, name, *rest):
            return [make(f"{name}{p}", *rest) for p in range(2)]

        ident = sb("a_ident", [P, P])
        wdkv = sb("a_wdkv", [P, DC, LAT])
        wuq = sb("a_wuq", [P, DC, D])
        wuk = sb("a_wuk", [LAT, D])
        wuv = sb("a_wuv", [LAT, D])
        x_in = pair(sb, "a_x", [P, TPC, D])
        stats = sb("a_stats", [P, TPC, 6])
        mean_var = sb("a_mv", [P, TPC, 2])
        var_eps = sb("a_var_eps", [P, TPC])
        inv_var = sb("a_inv_var", [P, TPC])
        root = sb("a_root", [P, TPC])
        newton = sb("a_newton", [P, TPC])
        rstd = sb("a_rstd", [P, TPC])
        xn = pair(sb, "a_xn", [P, TPC, D])
        xnT = sb("a_xnT", [P, DC, CHUNK])
        ckvT = sb("a_ckvT", [LAT, CHUNK])
        part = pair(sb, "a_part", [P, 2 * DC, PARTS, CHUNK], BF16)
        rest = pair(sb, "a_rest", [P, 2 * DC, CHUNK])
        v_out = pair(sb, "a_v", [P, TPC, D])

        tv_ps = ps("a_tv", [P, 2 * CHUNK])
        ckv_ps = ps("a_ckv", [P, CHUNK])
        qk_ps = ps("a_qk", [P, 2 * DC, CHUNK])

        w_in = sem("a_w_in")
        ident0 = sem("a_ident0")
        ident_ok = sem("a_ident_ok")
        x_ok = pair(sem, "a_x_ok")
        x_free = pair(sem, "a_x_free")
        ln_chain = sem("a_ln_chain")
        stats_turn = sem("a_stats_turn")
        root_ok = sem("a_root_ok")
        inv_var_ok = sem("a_inv_var_ok")
        xn_ok = pair(sem, "a_xn_ok")
        xT_ps_ok = sem("a_xT_ps_ok")
        xnT_ok = sem("a_xnT_ok")
        ckv_ps_ok = sem("a_ckv_ps_ok")
        ckvT_ok = sem("a_ckvT_ok")
        qk_ps_ok = sem("a_qk_ps_ok")
        v_ps_ok = sem("a_v_ps_ok")
        part1_ok = sem("a_part1_ok")
        rest_ok = sem("a_rest_ok")
        part2_ok = sem("a_part2_ok")
        part3_ok = sem("a_part3_ok")
        v_ok = sem("a_v_ok")
        part_out = pair(sem, "a_part_out")
        v_st = pair(sem, "a_v_st")
        block = ctx.enter_context(nc.Block())

        @block.sync
        def _(sp):
            sp.dma_start(wdkv[:], w_dkv.rearrange("(c p) n -> p c n", p=P)).then_inc(w_in, 16)
            sp.dma_start(wuq[:], w_uq.rearrange("(c p) n -> p c n", p=P)).then_inc(w_in, 16)
            sp.dma_start(wuk[:], w_uk).then_inc(w_in, 16)
            sp.dma_start(wuv[:], w_uv).then_inc(w_in, 16)
            with sp.Fori(0, NCHUNK // 2) as it:
                for p in range(2):
                    sp.wait_ge(x_free[p], it + 1)
                    sp.dma_start(x_in[p][:], x[bass.ds((it * 2 + p) * CHUNK, CHUNK), :].rearrange(
                        "(t p) d -> p t d", p=P)).then_inc(x_ok[p], 16)

        @block.gpsimd
        def _(pool):
            nc.gpsimd.memset(ident[:], 0.0).then_inc(ident0, 1)
            pool.wait_ge(ident0, 1)
            nc.gpsimd.affine_select(out=ident[:], in_=ident[:], compare_op=ALU.not_equal, fill=1.0, base=0,
                                    pattern=[[-1, P]], channel_multiplier=1).then_inc(ident_ok, 1)
            with pool.Fori(0, NCHUNK // 2) as it:
                for p in range(2):
                    pool.wait_ge(part2_ok, it * 2 + p + 1)
                    nc.gpsimd.tensor_tensor(part[p][:, :, 2, :], rest[p][:], part[p][:, :, 1, :],
                                            ALU.subtract).then_inc(part3_ok, 1)

        @block.scalar
        def _(act):
            with act.Fori(0, NCHUNK // 2) as it:
                for p in range(2):
                    act.wait_ge(inv_var_ok, it * 2 + p + 1)
                    nc.scalar.activation(root[:], inv_var[:], ACT.Sqrt).then_inc(root_ok, 1)
                    act.wait_ge(xT_ps_ok, it * 2 + p + 1)
                    nc.scalar.activation(xnT[:].rearrange("p c n -> p (c n)"), tv_ps[:],
                                         ACT.Copy).then_inc(xnT_ok, 1)
                    act.wait_ge(qk_ps_ok, it * 2 + p + 1)
                    act.wait_ge(part_out[p], (it + 1) * 32)
                    nc.scalar.activation(part[p][:, :, 0, :], qk_ps[:], ACT.Copy).then_inc(part1_ok, 1)
                    act.wait_ge(rest_ok, it * 2 + p + 2)
                    nc.scalar.activation(part[p][:, :, 1, :], rest[p][:], ACT.Copy).then_inc(part2_ok, 1)
                    act.wait_ge(part3_ok, it * 2 + p + 1)
                    for s, to in ((0, dram["q_parts"]), (1, dram["k_parts"])):
                        act.dma_start(to[:, :, :, bass.ds((it * 2 + p) * CHUNK, CHUNK)].rearrange(
                            "c g q n -> q c g n"), part[p][:, DC * s:DC * s + DC, :, :]).then_inc(part_out[p], 16)
                    act.wait_ge(v_ok, it * 2 + p + 2)
                    act.dma_start(dram["v"][bass.ds((it * 2 + p) * CHUNK, CHUNK), :].rearrange(
                        "(t p) d -> p t d", p=P), v_out[p][:]).then_inc(v_st[p], 16)
            for p in range(2):
                act.wait_ge(part_out[p], 32 * (NCHUNK // 2 + 1))
                act.wait_ge(v_st[p], 16 * (NCHUNK // 2 + 1))

        @block.vector
        def _(dve):
            for p in range(2):
                dve.sem_inc(x_free[p], 1)
                dve.sem_inc(part_out[p], 32)
                dve.sem_inc(v_st[p], 16)
            dve.sem_inc(rest_ok, 1)
            dve.sem_inc(v_ok, 1)
            with dve.Fori(0, NCHUNK // 2) as it:
                for p in range(2):
                    dve.wait_ge(x_ok[p], (it + 1) * 16)
                    dve.sem_inc(stats_turn, 1)
                    n = it * (2 * LN_STEPS) + p * LN_STEPS
                    for t in range(TPC):
                        last = nc.vector.bn_stats(stats[:, t, :], x_in[p][:, t, :])
                    last.then_inc(ln_chain, 1)
                    dve.wait_ge(ln_chain, n + 1)
                    dve.sem_inc(stats_turn, 1)
                    for t in range(TPC):
                        last = nc.vector.bn_aggr(mean_var[:, t, :], stats[:, t, :])
                    last.then_inc(ln_chain, 1)
                    dve.wait_ge(ln_chain, n + 2)
                    nc.vector.tensor_scalar(var_eps[:], mean_var[:, :, 1], EPS, None, ALU.add).then_inc(ln_chain, 1)
                    dve.wait_ge(ln_chain, n + 3)
                    nc.vector.reciprocal(inv_var[:], var_eps[:]).then_inc(inv_var_ok, 1)
                    dve.wait_ge(root_ok, it * 2 + p + 1)
                    nc.vector.tensor_tensor(newton[:], root[:], root[:], ALU.mult).then_inc(ln_chain, 1)
                    dve.wait_ge(ln_chain, n + 4)
                    nc.vector.tensor_tensor(newton[:], newton[:], var_eps[:], ALU.mult).then_inc(ln_chain, 1)
                    dve.wait_ge(ln_chain, n + 5)
                    nc.vector.tensor_scalar(newton[:], newton[:], -0.5, 1.5, ALU.mult, ALU.add).then_inc(ln_chain, 1)
                    dve.wait_ge(ln_chain, n + 6)
                    nc.vector.tensor_tensor(rstd[:], root[:], newton[:], ALU.mult).then_inc(ln_chain, 1)
                    dve.wait_ge(ln_chain, n + 7)
                    for t in range(TPC):
                        last = nc.vector.tensor_scalar(xn[p][:, t, :], x_in[p][:, t, :], mean_var[:, t, 0:1],
                                                       rstd[:, t:t + 1], ALU.subtract, ALU.mult)
                    last.then_inc(xn_ok[p], 1)
                    dve.wait_ge(xn_ok[p], it + 1)
                    dve.sem_inc(x_free[p], 1)
                    dve.wait_ge(ckv_ps_ok, it * 2 + p + 1)
                    nc.vector.tensor_copy(ckvT[:], ckv_ps[0:LAT, :]).then_inc(ckvT_ok, 1)
                    dve.wait_ge(part1_ok, it * 2 + p + 1)
                    nc.vector.tensor_tensor(rest[p][:], qk_ps[:], part[p][:, :, 0, :],
                                            ALU.subtract).then_inc(rest_ok, 1)
                    dve.wait_ge(v_ps_ok, it * 2 + p + 1)
                    dve.wait_ge(v_st[p], (it + 1) * 16)
                    nc.vector.tensor_copy(v_out[p][:].rearrange("p t d -> p (t d)"), tv_ps[:]).then_inc(v_ok, 1)

        @block.tensor
        def _(pe):
            pe.wait_ge(ident_ok, 1)
            pe.wait_ge(w_in, 64)
            with pe.Fori(0, NCHUNK // 2) as it:
                for p in range(2):
                    pe.wait_ge(xn_ok[p], it + 1)
                    pe.wait_ge(v_ok, it * 2 + p + 1)
                    for c in range(DC):
                        for t in range(TPC):
                            last = nc.tensor.transpose(tv_ps[:, c * CHUNK + t * P:c * CHUNK + (t + 1) * P],
                                                       xn[p][:, t, c * P:(c + 1) * P], ident[:])
                    last.then_inc(xT_ps_ok, 1)
                    pe.wait_ge(xnT_ok, it * 2 + p + 1)
                    for c in range(DC):
                        last = nc.tensor.matmul(ckv_ps[0:LAT, :], wdkv[:, c, :], xnT[:, c, :], start=(c == 0),
                                                stop=(c == DC - 1))
                    last.then_inc(ckv_ps_ok, 1)
                    pe.wait_ge(rest_ok, it * 2 + p + 1)
                    for m in range(DC):
                        for c in range(DC):
                            nc.tensor.matmul(qk_ps[:, m, :], wuq[:, c, m * P:(m + 1) * P], xnT[:, c, :],
                                             start=(c == 0), stop=(c == DC - 1))
                    pe.wait_ge(ckvT_ok, it * 2 + p + 1)
                    for m in range(DC):
                        last = nc.tensor.matmul(qk_ps[:, DC + m, :], wuk[:, m * P:(m + 1) * P], ckvT[:],
                                                start=True, stop=True)
                    last.then_inc(qk_ps_ok, 1)
                    for t in range(TPC):
                        last = nc.tensor.matmul(tv_ps[:, t * D:(t + 1) * D], ckvT[:, t * P:(t + 1) * P], wuv[:],
                                                start=True, stop=True)
                    last.then_inc(v_ps_ok, 1)


HALF = 512
PER_HALF = HALF // P
UNITS = QT + PER_HALF


def prob_unit(u):
    if u < PER_HALF:
        return u, 0, u * P, HALF - u * P, True
    j = u - PER_HALF
    first = max(0, (j - PER_HALF) * P)
    return j, 1, first, HALF - first, j >= PER_HALF


def max_unit(u):
    if u < PER_HALF:
        i = PER_HALF - 1 - u
        return i, 0, (i + 1) * P, True
    if u < QT:
        return u, 0, HALF, False
    i = PER_HALF + UNITS - 1 - u
    return i, 1, (i - PER_HALF + 1) * P, True


def attention_phase(nc, dram):
    RING = 4
    NM, NS = 2, 3
    NP = 12
    LAG = 2
    PER_QUAD = UNITS * QUAD
    HT = QUAD * QT
    with ExitStack() as ctx:
        def sb(name, shape, dt=F32):
            return ctx.enter_context(nc.sbuf_tensor(name, shape, dt))

        def ps(name, shape, dt=F32):
            return ctx.enter_context(nc.psum_tensor(name, shape, dt))

        def sem(name):
            return ctx.enter_context(nc.semaphore(name))

        def several(make, n, name, *rest):
            return [make(f"{name}{p}", *rest) for p in range(n)]

        ident = sb("b_ident", [P, P], BF16)
        mask_max = sb("b_mask_max", [P, P], BF16)
        mask_prob = sb("b_mask_prob", [P, P], BF16)
        q_st = several(sb, RING, "b_q_st", [P, QUAD, SEQ], BF16)
        k_st = several(sb, RING, "b_k_st", [P, QUAD, SEQ], BF16)
        v_in = several(sb, 2, "b_v_in", [P, QT, QUAD * HD])
        v_aug = several(sb, 2, "b_v_aug", [P, QT, QUAD, 2 * HD])
        prob = several(sb, NP, "b_prob", [P, HALF])
        neg_max = sb("b_neg_max", [P, 2, QUAD, QT])
        max_part = sb("b_max_part", [P, PARTS, HT], BF16)
        max_rest = sb("b_max_rest", [P, HT])
        max_rows = several(sb, 2, "b_max_rows", [PARTS * HT, P], BF16)
        ctx_out = several(sb, 2, "b_ctx_out", [P, SEQ])

        max_ps = several(ps, NM, "b_max_ps", [P, HALF])
        prob_ps = several(ps, NS, "b_prob_ps", [P, HALF])
        acc_ps = several(ps, 2, "b_acc_ps", [P, HALF])
        rows_ps = ps("b_rows_ps", [PARTS * HT, P], BF16)

        const0 = sem("b_const0")
        const_ok = sem("b_const_ok")
        ones_ok = sem("b_ones_ok")
        stack_ok = several(sem, RING, "b_stack_ok")
        v_in_ok = several(sem, 2, "b_v_in_ok")
        v_aug_ok = sem("b_v_aug_ok")
        max_sc_ok = sem("b_max_sc_ok")
        max_done = sem("b_max_done")
        chain = sem("b_chain")
        max_part_ok = sem("b_max_part_ok")
        rows_ps_ok = sem("b_rows_ps_ok")
        rows_ok = sem("b_rows_ok")
        rows_in = several(sem, RING, "b_rows_in")
        prob_sc_ok = sem("b_prob_sc_ok")
        prob_ok = sem("b_prob_ok")
        pv_ok = sem("b_pv_ok")
        acc_out = several(sem, 2, "b_acc_out")
        ctx_st = several(sem, 2, "b_ctx_st")
        block = ctx.enter_context(nc.Block())
        LOADS = 2 * len(Q_PART)

        @block.sync
        def _(sp):
            def load(g):
                b, w = divmod(g, RING)
                if g >= RING:
                    sp.wait_ge(prob_sc_ok, PER_QUAD * (g - RING + 1))
                for stack, parts, order in ((q_st[w], dram["q_parts"], Q_PART), (k_st[w], dram["k_parts"], K_PART)):
                    c, first = divmod(w * QUAD * HD, P)
                    for row, g3 in enumerate(order):
                        sp.dma_start(stack[row * HD:(row + 1) * HD, :, :],
                                     parts[c, g3, first:first + QUAD * HD, b * SEQ:(b + 1) * SEQ].rearrange(
                                         "(h r) n -> r h n", h=QUAD)).then_inc(
                            stack_ok[w], 16)
                if g >= 2:
                    sp.wait_ge(v_aug_ok, g - 1)
                sp.dma_start(v_in[g % 2][:], dram["v"].rearrange("(b t p) d -> b p t d", b=BATCH, p=P)[
                    b, :, :, w * QUAD * HD:(w + 1) * QUAD * HD]).then_inc(v_in_ok[g % 2], 16)

            def store(g):
                sp.wait_ge(acc_out[1], g + 1)
                sp.dma_start(dram["ctx"][g], ctx_out[g % 2][:]).then_inc(ctx_st[g % 2], 16)

            load(0)
            for s in range(-2, NQUAD + 1):
                if s + 3 < NQUAD:
                    load(s + 3)
                if s >= 1:
                    store(s - 1)
                if 0 <= s + 1 < NQUAD:
                    g = s + 1
                    sp.wait_ge(rows_ok, g + 1)
                    for n in range(PARTS):
                        sp.dma_start(q_st[g % RING][STACK + n:STACK + n + 1, :, :].rearrange("o h (t n) -> o (h t) n", n=P),
                                     max_rows[g % 2][n * HT:(n + 1) * HT, :]).then_inc(rows_in[g % RING], 16)
            for p in range(2):
                sp.wait_ge(ctx_st[p], 16 * (NQUAD // 2))

        @block.gpsimd
        def _(pool):
            for n, t in enumerate((ident, mask_max, mask_prob)):
                nc.gpsimd.memset(t[:], 0.0).then_inc(const0, 1)
            pool.wait_ge(const0, 3)
            nc.gpsimd.affine_select(out=ident[:], in_=ident[:], compare_op=ALU.not_equal, fill=1.0, base=0,
                                    pattern=[[-1, P]], channel_multiplier=1).then_inc(const_ok, 1)
            nc.gpsimd.affine_select(out=mask_max[:], in_=mask_max[:], compare_op=ALU.is_ge, fill=MASKED, base=0,
                                    pattern=[[-1, P]], channel_multiplier=1).then_inc(const_ok, 1)
            nc.gpsimd.affine_select(out=mask_prob[:], in_=mask_prob[:], compare_op=ALU.is_ge, fill=MASKED, base=0,
                                    pattern=[[1, P]], channel_multiplier=-1).then_inc(const_ok, 1)
            pool.wait_ge(ones_ok, RING + 2)
            for g in range(NQUAD):
                pool.wait_ge(v_in_ok[g % 2], 16 * (g // 2 + 1))
                if g >= 2:
                    pool.wait_ge(pv_ok, UNITS * (g - 1))
                nc.gpsimd.tensor_copy(v_aug[g % 2][:, :, :, 0:HD], v_in[g % 2][:].rearrange(
                    "p t (h r) -> p t h r", h=QUAD)).then_inc(v_aug_ok, 1)

        @block.vector
        def _(dve):
            for t in k_st:
                nc.vector.memset(t[STACK:P, :, :], 1.0).then_inc(ones_ok, 1)
            for t in v_aug:
                nc.vector.memset(t[:], 1.0).then_inc(ones_ok, 1)
            for g in range(NQUAD):
                for u in range(UNITS):
                    i, half, width, _ = max_unit(u)
                    for h in range(QUAD):
                        n = g * PER_QUAD + u * QUAD + h
                        dve.wait_ge(max_sc_ok, n + 1)
                        nc.vector.tensor_reduce(neg_max[:, half, h, i:i + 1], max_ps[n % NM][:, 0:width], AX.X,
                                                ALU.max, negate=True).then_inc(max_done, 1)
                dve.wait_ge(max_done, (g + 1) * PER_QUAD)
                both = neg_max[:, 0, :, PER_HALF:QT]
                nc.vector.tensor_tensor(both, both, neg_max[:, 1, :, PER_HALF:QT], ALU.min).then_inc(chain, 1)
                if g >= 1:
                    dve.wait_ge(rows_ps_ok, g)
                dve.wait_ge(chain, 4 * g + 1)
                whole = neg_max[:, 0, :, :].rearrange("p h t -> p (h t)")
                nc.vector.tensor_copy(max_part[:, 0, :], whole).then_inc(chain, 1)
                dve.wait_ge(chain, 4 * g + 2)
                nc.vector.tensor_tensor(max_rest[:], whole, max_part[:, 0, :], ALU.subtract).then_inc(chain, 1)
                dve.wait_ge(chain, 4 * g + 3)
                nc.vector.tensor_copy(max_part[:, 1, :], max_rest[:]).then_inc(chain, 1)
                dve.wait_ge(chain, 4 * g + 4)
                nc.vector.tensor_tensor(max_part[:, 2, :], max_rest[:], max_part[:, 1, :],
                                        ALU.subtract).then_inc(max_part_ok, 1)

        @block.scalar
        def _(act):
            def acc_copy(g, half):
                act.wait_ge(pv_ok, g * UNITS + (PER_HALF if half == 0 else UNITS))
                if g >= 2 and half == 0:
                    act.wait_ge(ctx_st[g % 2], 16 * (g // 2))
                nc.scalar.activation(ctx_out[g % 2][:, half * HALF:(half + 1) * HALF], acc_ps[half][:],
                                     ACT.Copy).then_inc(acc_out[half], 1)

            def rows_copy(g):
                act.wait_ge(rows_ps_ok, g + 1)
                if g >= 2:
                    act.wait_ge(rows_in[(g - 2) % RING], 16 * PARTS * ((g - 2) // RING + 1))
                nc.scalar.activation(max_rows[g % 2][:], rows_ps[:], ACT.Copy).then_inc(rows_ok, 1)

            for s in range(-2, NQUAD):
                if s < 0:
                    if s + 1 >= 0:
                        rows_copy(s + 1)
                    continue
                for u in range(UNITS):
                    _, _, _, width, _ = prob_unit(u)
                    if u == 2 and s >= 1:
                        acc_copy(s - 1, 1)
                    if u == 4 and s + 1 < NQUAD:
                        rows_copy(s + 1)
                    if u == PER_HALF + LAG:
                        acc_copy(s, 0)
                    for h in range(QUAD):
                        n = s * PER_QUAD + u * QUAD + h
                        act.wait_ge(prob_sc_ok, n + 1)
                        if n >= NP:
                            act.wait_ge(pv_ok, (n - NP) // QUAD + 1)
                        nc.scalar.activation(prob[n % NP][:, 0:width], prob_ps[n % NS][:, 0:width], ACT.Exp,
                                             scale=SCALE).then_inc(prob_ok, 1)
            acc_copy(NQUAD - 1, 1)

        @block.tensor
        def _(pe):
            def max_scores(g, u, h):
                i, half, width, diagonal = max_unit(u)
                n = g * PER_QUAD + u * QUAD + h
                if u == 0 and h == 0:
                    pe.wait_ge(stack_ok[g % RING], 16 * LOADS * (g // RING + 1))
                if n >= NM:
                    pe.wait_ge(max_done, n - NM + 1)
                out = max_ps[n % NM]
                mm = nc.tensor.matmul(out[:, 0:width], q_st[g % RING][0:STACK, h, i * P:(i + 1) * P],
                                      k_st[g % RING][0:STACK, h, half * HALF:half * HALF + width],
                                      start=True, stop=not diagonal)
                if diagonal:
                    mm = nc.tensor.matmul(out[:, width - P:width], ident[:], mask_max[:], start=False, stop=True)
                mm.then_inc(max_sc_ok, 1)

            def prob_scores(g, u, h):
                j, half, first, width, diagonal = prob_unit(u)
                n = g * PER_QUAD + u * QUAD + h
                if u == 0 and h == 0:
                    pe.wait_ge(rows_in[g % RING], 16 * PARTS * (g // RING + 1))
                if n >= NS:
                    pe.wait_ge(prob_ok, n - NS + 1)
                out = prob_ps[n % NS]
                q0 = half * HALF + first
                mm = nc.tensor.matmul(out[:, 0:width], k_st[g % RING][0:MAXROWS, h, j * P:(j + 1) * P],
                                      q_st[g % RING][0:MAXROWS, h, q0:q0 + width], start=True, stop=not diagonal)
                if diagonal:
                    mm = nc.tensor.matmul(out[:, 0:P], ident[:], mask_prob[:], start=False, stop=True)
                mm.then_inc(prob_sc_ok, 1)

            def products(unit):
                g, u = divmod(unit, UNITS)
                j, half, first, width, _ = prob_unit(u)
                if u == 0:
                    pe.wait_ge(v_aug_ok, g + 1)
                if j == 0 and g >= 1:
                    pe.wait_ge(acc_out[half], g)
                pe.wait_ge(prob_ok, QUAD * (unit + 1))
                for h in range(QUAD):
                    mm = nc.tensor.matmul(acc_ps[half][32 * h:32 * h + 2 * HD, first:first + width],
                                          v_aug[g % 2][:, j, h, :], prob[(unit * QUAD + h) % NP][:, 0:width],
                                          start=(j == 0), stop=(j == (PER_HALF if half == 0 else QT) - 1),
                                          tile_position=(0, 32 * h))
                mm.then_inc(pv_ok, 1)

            def max_rows_transposed(g):
                pe.wait_ge(max_part_ok, g + 1)
                if g >= 1:
                    pe.wait_ge(rows_ok, g)
                nc.tensor.transpose(rows_ps[:], max_part[:].rearrange("p a n -> p (a n)"), ident[:]).then_inc(
                    rows_ps_ok, 1)

            pe.wait_ge(const_ok, 3)
            pe.wait_ge(ones_ok, RING + 2)
            for s in range(-2, NQUAD):
                for u in range(UNITS):
                    if u == 3 and 0 <= s + 1 < NQUAD:
                        max_rows_transposed(s + 1)
                    for h in range(QUAD):
                        if s + 2 < NQUAD:
                            max_scores(s + 2, u, h)
                        if s >= 0:
                            prob_scores(s, u, h)
                    unit = s * UNITS + u - LAG
                    if unit >= 0:
                        products(unit)
            for unit in range(NQUAD * UNITS - LAG, NQUAD * UNITS):
                products(unit)


EXPERTS, TOP, FF = 8, 2, 512
FC = FF // P
BT = SEQ // P
SLOT_TILES = (TOP * NTOK + EXPERTS * (P - 1)) // P
SLOT_UNROLL = 4
SLOT_TILES += -SLOT_TILES % SLOT_UNROLL


def mixed_phase(nc, dram, x, w_o, w_r, temp, w1, b1, w2, b2, out):
    with ExitStack() as ctx:
        def sb(name, shape, dt=F32):
            return ctx.enter_context(nc.sbuf_tensor(name, shape, dt))

        x2 = sb("m_x2", [P, NTILE, D])
        weight = sb("m_weight", [P, TOP, NTILE])
        slot = sb("m_slot", [P, TOP, NTILE], I32)
        tile_expert = sb("m_tile_expert", [1, SLOT_TILES], I32)
        with ExitStack() as inner:
            xn2 = inner.enter_context(nc.sbuf_tensor("m_xn2", [P, NTILE, D], F32))
            logits = inner.enter_context(nc.sbuf_tensor("m_logits", [P, NTILE, EXPERTS], F32))
            output_projection_phase(nc, dram, x, w_o, w_r, temp, x2, xn2, logits)
            routing_phase(nc, dram, xn2, logits, weight, slot, tile_expert)
        expert_phase(nc, dram, w1, b1, w2, b2, tile_expert)
        combine_phase(nc, dram, x2, weight, slot, out)


def output_projection_phase(nc, dram, x, w_o, w_r, temp, x2, xn2, logits):
    with ExitStack() as ctx:
        def sb(name, shape, dt=F32):
            return ctx.enter_context(nc.sbuf_tensor(name, shape, dt))

        def ps(name, shape, dt=F32):
            return ctx.enter_context(nc.psum_tensor(name, shape, dt))

        def sem(name):
            return ctx.enter_context(nc.semaphore(name))

        QUADS = HEADS // QUAD
        ident = sb("c_ident", [P, P])
        wo = sb("c_wo", [P, DC, D])
        wr = sb("c_wr", [P, DC, EXPERTS])
        temp_in = sb("c_temp", [P, 1])
        inv_temp = sb("c_inv_temp", [P, 1])
        ctx_in = sb("c_ctx_in", [P, QUADS, SEQ])
        x_in = sb("c_x_in", [P, BT, D])
        inv_den = [sb(f"c_inv_den{n}", [P, HEADS]) for n in range(2)]
        heads = [sb(f"c_heads{n}", [P, D]) for n in range(2)]
        headsT = [sb(f"c_headsT{n}", [P, D]) for n in range(2)]
        stats = sb("c_stats", [P, BT, 6])
        mean_var = sb("c_mv", [P, BT, 2])
        var_eps = sb("c_var_eps", [P, BT])
        inv_var = sb("c_inv_var", [P, BT])
        root = sb("c_root", [P, BT])
        newton = sb("c_newton", [P, BT])
        rstd = sb("c_rstd", [P, BT])
        xn = sb("c_xn", [P, BT, D])
        xnT = [sb(f"c_xnT{n}", [P, DC, P]) for n in range(2)]

        rows_ps = [ps(f"c_rows_ps{n}", [P, QUADS, P]) for n in range(2)]
        headsT_ps = [ps(f"c_headsT_ps{n}", [P, D]) for n in range(2)]
        proj_ps = [ps(f"c_proj_ps{n}", [P, D]) for n in range(2)]
        logit_ps = ps("c_logit_ps", [P, BT, EXPERTS])

        w_in = sem("c_w_in")
        ident0 = sem("c_ident0")
        ident_ok = sem("c_ident_ok")
        inv_temp_ok = sem("c_inv_temp_ok")
        in_ok = sem("c_in_ok")
        ctx_read = sem("c_ctx_read")
        rows_ok = sem("c_rows_ok")
        inv_den_ok = sem("c_inv_den_ok")
        heads_ok = sem("c_heads_ok")
        headsT_ps_ok = sem("c_headsT_ps_ok")
        headsT_ok = sem("c_headsT_ok")
        proj_ok = sem("c_proj_ok")
        x2_ok = sem("c_x2_ok")
        ln_chain = sem("c_ln_chain")
        stats_turn = sem("c_stats_turn")
        inv_var_ok = sem("c_inv_var_ok")
        root_ok = sem("c_root_ok")
        ln_rstd_ok = sem("c_ln_rstd_ok")
        xn_ok = sem("c_xn_ok")
        xn_kept = sem("c_xn_kept")
        xnT_ps_ok = sem("c_xnT_ps_ok")
        xnT_ok = sem("c_xnT_ok")
        logit_ps_ok = sem("c_logit_ps_ok")
        logit_ok = sem("c_logit_ok")
        block = ctx.enter_context(nc.Block())
        LN = 6

        @block.sync
        def _(sp):
            sp.dma_start(wo[:], w_o.rearrange("(c p) n -> p c n", p=P)).then_inc(w_in, 16)
            sp.dma_start(wr[:], w_r.rearrange("(c p) n -> p c n", p=P)).then_inc(w_in, 16)
            sp.dma_start(temp_in[:], temp.rearrange("(o n) -> o n", o=1).to_broadcast([P, 1])).then_inc(w_in, 16)
            with sp.Fori(0, BATCH) as it:
                sp.wait_ge(ctx_read, it + 1)
                sp.dma_start(ctx_in[:], dram["ctx"][bass.ds(it * QUADS, QUADS), :, :].rearrange(
                    "g p n -> p g n")).then_inc(in_ok, 16)
                sp.wait_ge(x2_ok, it * BT + 1)
                sp.dma_start(x_in[:], x[bass.ds(it * SEQ, SEQ), :].rearrange("(t p) d -> p t d", p=P)).then_inc(
                    in_ok, 16)

        @block.gpsimd
        def _(pool):
            nc.gpsimd.memset(ident[:], 0.0).then_inc(ident0, 1)
            pool.wait_ge(ident0, 1)
            nc.gpsimd.affine_select(out=ident[:], in_=ident[:], compare_op=ALU.not_equal, fill=1.0, base=0,
                                    pattern=[[-1, P]], channel_multiplier=1).then_inc(ident_ok, 1)

        @block.vector
        def _(dve):
            dve.sem_inc(ctx_read, 1)
            dve.sem_inc(x2_ok, 1)
            dve.sem_inc(xn_kept, 1)
            dve.sem_inc(logit_ok, 1)
            dve.wait_ge(w_in, 48)
            nc.vector.reciprocal(inv_temp[:], temp_in[:]).then_inc(inv_temp_ok, 1)
            dve.wait_ge(inv_temp_ok, 1)
            with dve.Fori(0, BATCH) as it:
                def normalise(t):
                    n = it * BT + t
                    view = rows_ps[t % 2][:].rearrange("p g (h s r) -> p (g h) s r", h=QUAD, s=2)
                    dve.wait_ge(rows_ok, n + 1)
                    nc.vector.reciprocal(inv_den[t % 2][:], view[:, :, 1, 0]).then_inc(inv_den_ok, 1)
                    dve.wait_ge(inv_den_ok, n + 1)
                    nc.vector.tensor_tensor(heads[t % 2][:].rearrange("p (h r) -> p h r", r=HD), view[:, :, 0, :],
                                            inv_den[t % 2][:].unsqueeze(2).to_broadcast([P, HEADS, HD]),
                                            ALU.mult).then_inc(heads_ok, 1)

                def residual(t):
                    n = it * BT + t
                    dve.wait_ge(proj_ok, n + 1)
                    nc.vector.tensor_tensor(x2[:, bass.ds(n, 1), :].rearrange("p o d -> p (o d)"), proj_ps[t % 2][:],
                                            x_in[:, t, :], ALU.add).then_inc(x2_ok, 1)

                dve.wait_ge(in_ok, (it + 1) * 32)
                for t in range(BT + 2):
                    if t < BT:
                        normalise(t)
                    if t >= 2:
                        residual(t - 2)
                dve.wait_ge(x2_ok, it * BT + BT + 1)
                dve.sem_inc(stats_turn, 1)
                n = it * LN
                for t in range(BT):
                    last = nc.vector.bn_stats(stats[:, t, :], x2[:, bass.ds(it * BT + t, 1), :].rearrange(
                        "p o d -> p (o d)"))
                last.then_inc(ln_chain, 1)
                dve.wait_ge(ln_chain, n + 1)
                dve.sem_inc(stats_turn, 1)
                for t in range(BT):
                    last = nc.vector.bn_aggr(mean_var[:, t, :], stats[:, t, :])
                last.then_inc(ln_chain, 1)
                dve.wait_ge(ln_chain, n + 2)
                nc.vector.tensor_scalar(var_eps[:], mean_var[:, :, 1], EPS, None, ALU.add).then_inc(ln_chain, 1)
                dve.wait_ge(ln_chain, n + 3)
                nc.vector.reciprocal(inv_var[:], var_eps[:]).then_inc(inv_var_ok, 1)
                dve.wait_ge(root_ok, it + 1)
                nc.vector.tensor_tensor(newton[:], root[:], root[:], ALU.mult).then_inc(ln_chain, 1)
                dve.wait_ge(ln_chain, n + 4)
                nc.vector.tensor_tensor(newton[:], newton[:], var_eps[:], ALU.mult).then_inc(ln_chain, 1)
                dve.wait_ge(ln_chain, n + 5)
                nc.vector.tensor_scalar(newton[:], newton[:], -0.5, 1.5, ALU.mult, ALU.add).then_inc(ln_chain, 1)
                dve.wait_ge(ln_chain, n + 6)
                nc.vector.tensor_tensor(rstd[:], root[:], newton[:], ALU.mult).then_inc(ln_rstd_ok, 1)
                dve.wait_ge(ln_rstd_ok, it + 1)
                dve.wait_ge(xn_kept, it + 1)
                for t in range(BT):
                    last = nc.vector.tensor_scalar(xn[:, t, :], x2[:, bass.ds(it * BT + t, 1), :].rearrange(
                        "p o d -> p (o d)"), mean_var[:, t, 0:1], rstd[:, t:t + 1], ALU.subtract, ALU.mult)
                last.then_inc(xn_ok, 1)
                dve.wait_ge(logit_ps_ok, it + 1)
                nc.vector.tensor_scalar(logits[:, bass.ds(it * BT, BT), :], logit_ps[:], inv_temp[:, 0:1], None,
                                        ALU.mult).then_inc(logit_ok, 1)

        @block.scalar
        def _(act):
            with act.Fori(0, BATCH) as it:
                for t in range(BT):
                    act.wait_ge(headsT_ps_ok, it * BT + t + 1)
                    nc.scalar.activation(headsT[t % 2][:], headsT_ps[t % 2][:], ACT.Copy).then_inc(headsT_ok, 1)
                act.wait_ge(inv_var_ok, it + 1)
                nc.scalar.activation(root[:], inv_var[:], ACT.Sqrt).then_inc(root_ok, 1)
                act.wait_ge(xn_ok, it + 1)
                nc.scalar.activation(xn2[:, bass.ds(it * BT, BT), :], xn[:], ACT.Copy).then_inc(xn_kept, 1)
                for t in range(BT):
                    act.wait_ge(xnT_ps_ok, it * BT + t + 1)
                    nc.scalar.activation(xnT[t % 2][:].rearrange("p c n -> p (c n)"), headsT_ps[t % 2][:],
                                         ACT.Copy).then_inc(xnT_ok, 1)

        @block.tensor
        def _(pe):
            pe.wait_ge(ident_ok, 1)
            pe.wait_ge(w_in, 48)
            with pe.Fori(0, BATCH) as it:
                def rows(t):
                    if t >= 2:
                        pe.wait_ge(heads_ok, it * BT + t - 1)
                    for g in range(QUADS):
                        last = nc.tensor.transpose(rows_ps[t % 2][:, g, :], ctx_in[:, g, t * P:(t + 1) * P], ident[:])
                    last.then_inc(rows_ok, 1)

                def turned(t):
                    pe.wait_ge(heads_ok, it * BT + t + 1)
                    if t >= 2:
                        pe.wait_ge(headsT_ok, it * BT + t - 1)
                    for c in range(DC):
                        last = nc.tensor.transpose(headsT_ps[t % 2][:, c * P:(c + 1) * P],
                                                   heads[t % 2][:, c * P:(c + 1) * P], ident[:])
                    last.then_inc(headsT_ps_ok, 1)

                def project(t):
                    pe.wait_ge(headsT_ok, it * BT + t + 1)
                    if t >= 2:
                        pe.wait_ge(x2_ok, it * BT + t)
                    for c in range(DC):
                        last = nc.tensor.matmul(proj_ps[t % 2][:], headsT[t % 2][:, c * P:(c + 1) * P], wo[:, c, :],
                                                start=(c == 0), stop=(c == DC - 1))
                    last.then_inc(proj_ok, 1)

                pe.wait_ge(in_ok, (it + 1) * 32)
                for t in range(BT + 2):
                    if t < BT:
                        rows(t)
                    if t == BT - 1:
                        pe.wait_ge(rows_ok, it * BT + BT)
                        pe.sem_inc(ctx_read, 1)
                    if 1 <= t <= BT:
                        turned(t - 1)
                    if t >= 2:
                        project(t - 2)
                pe.wait_ge(xn_ok, it + 1)
                pe.wait_ge(logit_ok, it + 1)
                for t in range(BT + 1):
                    if t < BT:
                        if t >= 2:
                            pe.wait_ge(xnT_ok, it * BT + t - 1)
                        for c in range(DC):
                            last = nc.tensor.transpose(headsT_ps[t % 2][:, c * P:(c + 1) * P],
                                                       xn[:, t, c * P:(c + 1) * P], ident[:])
                        last.then_inc(xnT_ps_ok, 1)
                    if t >= 1:
                        pe.wait_ge(xnT_ok, it * BT + t)
                        for c in range(DC):
                            last = nc.tensor.matmul(logit_ps[:, t - 1, :], xnT[(t - 1) % 2][:, c, :], wr[:, c, :],
                                                    start=(c == 0), stop=(c == DC - 1))
                last.then_inc(logit_ps_ok, 1)


def routing_phase(nc, dram, xn2, logits, weight, slot, tile_expert):
    BIG = 3.0e38
    with ExitStack() as ctx:
        def sb(name, shape, dt=F32):
            return ctx.enter_context(nc.sbuf_tensor(name, shape, dt))

        def sem(name):
            return ctx.enter_context(nc.semaphore(name))

        shape = [P, NTILE, EXPERTS]
        order = sb("r_order", shape)
        rank = sb("r_rank", shape)
        second = sb("r_second", shape)
        one_hot = [sb(f"r_one_hot{k}", shape) for k in range(TOP)]
        top = [sb(f"r_top{k}", [P, NTILE]) for k in range(TOP)]
        key = sb("r_key", [P, NTILE])
        power = sb("r_power", [P, NTILE])
        total = sb("r_total", [P, NTILE])
        chosen = sb("r_chosen", [P, EXPERTS, NTILE], BF16)
        before = sb("r_before", [P, P], BF16)
        ones = sb("r_ones", [P, P], BF16)
        ones_row = sb("r_ones_row", [P, EXPERTS * NTILE])
        tile_index = sb("r_tile_index", [P, SLOT_TILES, EXPERTS])
        running = sb("r_running", [P, EXPERTS, NTILE])
        place = sb("r_place", [P, EXPERTS, NTILE])
        count = sb("r_count", [P, EXPERTS])
        count_i = sb("r_count_i", [P, EXPERTS], I32)
        tiles_i = sb("r_tiles_i", [P, EXPERTS], I32)
        tiles = sb("r_tiles", [P, EXPERTS])
        tiles_end = sb("r_tiles_end", [P, EXPERTS])
        base = sb("r_base", [P, EXPERTS])
        picked = sb("r_picked", shape)
        slot_f = [sb(f"r_slot_f{k}", [P, NTILE]) for k in range(TOP)]
        passed = sb("r_passed", [P, SLOT_TILES, EXPERTS])
        tile_f = sb("r_tile_f", [P, SLOT_TILES])
        prefix_ps = ctx.enter_context(nc.psum_tensor("r_prefix_ps", [P, EXPERTS, NTILE], F32))
        total_ps = ctx.enter_context(nc.psum_tensor("r_total_ps", [P, EXPERTS, NTILE], F32))
        const_ok = sem("r_const_ok")
        before0 = sem("r_before0")
        step = sem("r_step")
        gap_ok = sem("r_gap_ok")
        power_ok = sem("r_power_ok")
        chosen_ok = sem("r_chosen_ok")
        counts_ok = sem("r_counts_ok")
        slot_ok = sem("r_slot_ok")
        scattered = sem("r_scattered")
        block = ctx.enter_context(nc.Block())

        @block.gpsimd
        def _(pool):
            nc.gpsimd.iota(order[:], [[0, NTILE], [-1, EXPERTS]], base=EXPERTS, channel_multiplier=0,
                           allow_small_or_imprecise_dtypes=True).then_inc(const_ok, 1)
            nc.gpsimd.iota(tile_index[:], [[1, SLOT_TILES], [0, EXPERTS]], base=0, channel_multiplier=0,
                           allow_small_or_imprecise_dtypes=True).then_inc(const_ok, 1)
            nc.gpsimd.memset(before[:], 1.0).then_inc(before0, 1)
            pool.wait_ge(before0, 1)
            nc.gpsimd.affine_select(out=before[:], in_=before[:], compare_op=ALU.is_gt, fill=0.0, base=0,
                                    pattern=[[1, P]], channel_multiplier=-1).then_inc(const_ok, 1)
            pool.wait_ge(slot_ok, 1)
            for k in range(TOP):
                for t in range(NTILE):
                    nc.gpsimd.indirect_dma_start(
                        out=dram["rows"], out_offset=bass.IndirectOffsetOnAxis(ap=slot[:, k, t:t + 1], axis=0),
                        in_=xn2[:, t, :], in_offset=None).then_inc(scattered, 16)
            pool.wait_ge(scattered, 16 * TOP * NTILE)

        @block.scalar
        def _(act):
            act.wait_ge(gap_ok, 1)
            nc.scalar.activation(power[:], key[:], ACT.Exp).then_inc(power_ok, 1)

        @block.tensor
        def _(pe):
            pe.wait_ge(const_ok, 3)
            pe.wait_ge(chosen_ok, 1)
            flat = chosen[:].rearrange("p e t -> p (e t)")
            nc.tensor.matmul(prefix_ps[:].rearrange("p e t -> p (e t)"), before[:], flat, start=True, stop=True)
            nc.tensor.matmul(total_ps[:].rearrange("p e t -> p (e t)"), ones[:], flat, start=True,
                             stop=True).then_inc(counts_ok, 1)

        @block.vector
        def _(dve):
            done = [0]

            def then(ins):
                done[0] += 1
                ins.then_inc(step, 1)
                dve.wait_ge(step, done[0])

            def wide(ap, n=EXPERTS):
                return ap.unsqueeze(2).to_broadcast([P, ap.shape[1], n])

            nc.vector.memset(ones[:], 1.0)
            then(nc.vector.memset(ones_row[:], 1.0))
            dve.wait_ge(const_ok, 3)
            values = logits
            for k in range(TOP):
                then(nc.vector.tensor_reduce(top[k][:], values[:], AX.X, ALU.max))
                then(nc.vector.tensor_tensor(rank[:], values[:], wide(top[k][:]), ALU.is_equal))
                then(nc.vector.tensor_tensor(rank[:], rank[:], order[:], ALU.mult))
                then(nc.vector.tensor_reduce(key[:], rank[:], AX.X, ALU.max))
                then(nc.vector.tensor_tensor(one_hot[k][:], order[:], wide(key[:]), ALU.is_equal))
                if k == 0:
                    then(nc.vector.tensor_scalar(second[:], one_hot[0][:], -2 * BIG / 2, BIG / 2, ALU.mult, ALU.add))
                    then(nc.vector.tensor_tensor(second[:], second[:], logits[:], ALU.min))
                    values = second
            dve_gap = nc.vector.tensor_tensor(key[:], top[1][:], top[0][:], ALU.subtract)
            dve_gap.then_inc(gap_ok, 1)
            then(nc.vector.tensor_tensor(chosen[:].rearrange("p e t -> p t e"), one_hot[0][:], one_hot[1][:], ALU.add))
            dve.sem_inc(chosen_ok, 1)
            dve.wait_ge(power_ok, 1)
            then(nc.vector.tensor_scalar(total[:], power[:], 1.0, None, ALU.add))
            then(nc.vector.reciprocal(weight[:, 0, :], total[:]))
            then(nc.vector.tensor_tensor(weight[:, 1, :], power[:], weight[:, 0, :], ALU.mult))
            dve.wait_ge(counts_ok, 1)
            then(nc.vector.tensor_tensor_scan(running[:].rearrange("p e t -> p (e t)"), ones_row[:],
                                              total_ps[:].rearrange("p e t -> p (e t)"), 0.0, ALU.mult, ALU.add))
            then(nc.vector.tensor_tensor(place[:], running[:], total_ps[:], ALU.subtract))
            then(nc.vector.tensor_tensor(count[:], running[:, :, NTILE - 1], place[:, :, 0], ALU.subtract))
            then(nc.vector.tensor_scalar(count_i[:], count[:], float(P - 1), None, ALU.add))
            then(nc.vector.tensor_scalar(tiles_i[:], count_i[:], P.bit_length() - 1, None, ALU.logical_shift_right))
            then(nc.vector.tensor_copy(tiles[:], tiles_i[:]))
            then(nc.vector.tensor_tensor_scan(tiles_end[:], ones_row[:, 0:EXPERTS], tiles[:], 0.0, ALU.mult, ALU.add))
            then(nc.vector.tensor_tensor(base[:], tiles_end[:], tiles[:], ALU.subtract))
            then(nc.vector.scalar_tensor_tensor(out=base[:], in0=base[:], scalar=float(P), in1=place[:, :, 0],
                                                op0=ALU.mult, op1=ALU.subtract))
            then(nc.vector.tensor_tensor(place[:], place[:], wide(base[:], NTILE), ALU.add))
            then(nc.vector.tensor_tensor(place[:], place[:], prefix_ps[:], ALU.add))
            for k in range(TOP):
                then(nc.vector.tensor_tensor(picked[:], one_hot[k][:], place[:].rearrange("p e t -> p t e"), ALU.mult))
                then(nc.vector.tensor_reduce(slot_f[k][:], picked[:], AX.X, ALU.add))
                then(nc.vector.tensor_copy(slot[:, k, :], slot_f[k][:]))
            dve.sem_inc(slot_ok, 1)
            then(nc.vector.tensor_tensor(passed[:], tile_index[:],
                                         tiles_end[:].unsqueeze(1).to_broadcast([P, SLOT_TILES, EXPERTS]), ALU.is_ge))
            then(nc.vector.tensor_reduce(tile_f[:], passed[:], AX.X, ALU.add))
            then(nc.vector.tensor_scalar(tile_expert[:], tile_f[0:1, :], float(EXPERTS - 1), None, ALU.min))


def expert_phase(nc, dram, w1, b1, w2, b2, tile_expert):
    with ExitStack() as ctx:
        def sb(name, shape, dt=F32):
            return ctx.enter_context(nc.sbuf_tensor(name, shape, dt))

        def ps(name, shape, dt=F32):
            return ctx.enter_context(nc.psum_tensor(name, shape, dt))

        def sem(name):
            return ctx.enter_context(nc.semaphore(name))

        U = SLOT_UNROLL
        H1, H2 = 2 * FF * EXPERTS, D * EXPERTS
        ident = sb("e_ident", [P, P])
        w1_sb = sb("e_w1", [P, EXPERTS, DC, 2 * FF])
        w2_sb = sb("e_w2", [P, EXPERTS, FC, D])
        bias_in = [sb("e_b1_in", [P, H1 // P]), sb("e_b2_in", [P, H2 // P])]
        bias_rest = [sb("e_b1_rest", [P, H1 // P]), sb("e_b2_rest", [P, H2 // P])]
        bias_part = [sb("e_b1_part", [P, PARTS, H1 // P], BF16), sb("e_b2_part", [P, PARTS, H2 // P], BF16)]
        bias = [sb("e_b1", [PARTS, EXPERTS, 2 * FF], BF16), sb("e_b2", [PARTS, EXPERTS, D], BF16)]
        ones = sb("e_ones", [PARTS, P], BF16)
        rows = [sb(f"e_rows{n}", [P, D]) for n in range(U)]
        rowsT = [sb(f"e_rowsT{n}", [P, D]) for n in range(2)]
        gate = [sb(f"e_gate{n}", [P, FF]) for n in range(2)]
        hidden = [sb(f"e_hidden{n}", [P, FF]) for n in range(2)]
        hiddenT = [sb(f"e_hiddenT{n}", [P, FF]) for n in range(2)]
        y = [sb(f"e_y{n}", [P, D]) for n in range(U)]

        rowsT_ps = ps("e_rowsT_ps", [P, D])
        a_ps = [ps(f"e_a_ps{n}", [P, FF]) for n in range(2)]
        g_ps = [ps(f"e_g_ps{n}", [P, FF]) for n in range(2)]
        hiddenT_ps = ps("e_hiddenT_ps", [P, FF])
        y_ps = [ps(f"e_y_ps{n}", [P, D]) for n in range(2)]

        ident0 = sem("e_ident0")
        ident_ok = sem("e_ident_ok")
        w_in = sem("e_w_in")
        bias_in_ok = sem("e_bias_in_ok")
        chain = sem("e_chain")
        bias_ok = sem("e_bias_ok")
        ones_ok = sem("e_ones_ok")
        rows_ok = [sem(f"e_rows_ok{n}") for n in range(U)]
        rowsT_ps_ok = sem("e_rowsT_ps_ok")
        rowsT_ok = sem("e_rowsT_ok")
        g_ok = sem("e_g_ok")
        a_ok = sem("e_a_ok")
        gate_ok = sem("e_gate_ok")
        hidden_ok = sem("e_hidden_ok")
        hiddenT_ps_ok = sem("e_hiddenT_ps_ok")
        hiddenT_ok = sem("e_hiddenT_ok")
        y_ps_ok = sem("e_y_ps_ok")
        y_ok = sem("e_y_ok")
        y_st = [sem(f"e_y_st{n}") for n in range(U)]
        block = ctx.enter_context(nc.Block())

        @block.sync
        def _(sp):
            sp.dma_start(bias_in[0][:], b1.rearrange("e (q n) -> (e q) n", n=H1 // P)).then_inc(bias_in_ok, 16)
            sp.dma_start(bias_in[1][:], b2.rearrange("e (q n) -> (e q) n", n=H2 // P)).then_inc(bias_in_ok, 16)
            for e in range(EXPERTS):
                sp.dma_start(w1_sb[:, e, :, :], w1[e].rearrange("(c p) n -> p c n", p=P)).then_inc(w_in, 16)
                sp.dma_start(w2_sb[:, e, :, :], w2[e].rearrange("(c p) n -> p c n", p=P)).then_inc(w_in, 16)
            sp.wait_ge(chain, 2 * 5)
            for n in range(2):
                for q in range(PARTS):
                    sp.dma_start(bias[n][q:q + 1, :, :].rearrange("o e n -> o (e n)").rearrange(
                        "o (p n) -> o p n", p=P), bias_part[n][:, q, :]).then_inc(bias_ok, 16)
            with sp.Fori(0, SLOT_TILES // U) as it:
                for t in range(U):
                    sp.wait_ge(rowsT_ps_ok, it * U + t + 1)
                    sp.dma_start(rows[t][:], dram["rows"][bass.ds((it * U + t) * P, P), :]).then_inc(rows_ok[t], 16)

        @block.gpsimd
        def _(pool):
            nc.gpsimd.memset(ident[:], 0.0).then_inc(ident0, 1)
            pool.wait_ge(ident0, 1)
            nc.gpsimd.affine_select(out=ident[:], in_=ident[:], compare_op=ALU.not_equal, fill=1.0, base=0,
                                    pattern=[[-1, P]], channel_multiplier=1).then_inc(ident_ok, 1)

        @block.vector
        def _(dve):
            nc.vector.memset(ones[:], 1.0).then_inc(ones_ok, 1)
            dve.wait_ge(bias_in_ok, 32)
            for n in range(2):
                whole, rest, part = bias_in[n], bias_rest[n], bias_part[n]
                nc.vector.tensor_copy(part[:, 0, :], whole[:]).then_inc(chain, 1)
                dve.wait_ge(chain, 5 * n + 1)
                nc.vector.tensor_tensor(rest[:], whole[:], part[:, 0, :], ALU.subtract).then_inc(chain, 1)
                dve.wait_ge(chain, 5 * n + 2)
                nc.vector.tensor_copy(part[:, 1, :], rest[:]).then_inc(chain, 1)
                dve.wait_ge(chain, 5 * n + 3)
                nc.vector.tensor_tensor(rest[:], rest[:], part[:, 1, :], ALU.subtract).then_inc(chain, 1)
                dve.wait_ge(chain, 5 * n + 4)
                nc.vector.tensor_copy(part[:, 2, :], rest[:]).then_inc(chain, 1)
            with dve.Fori(0, SLOT_TILES // U) as it:
                def gated(t):
                    dve.wait_ge(a_ok, it * U + t + 1)
                    dve.wait_ge(gate_ok, it * U + t + 1)
                    nc.vector.tensor_tensor(hidden[t % 2][:], a_ps[t % 2][:], gate[t % 2][:],
                                            ALU.mult).then_inc(hidden_ok, 1)

                def turned(t):
                    dve.wait_ge(hiddenT_ps_ok, it * U + t + 1)
                    nc.vector.tensor_copy(hiddenT[t % 2][:], hiddenT_ps[:]).then_inc(hiddenT_ok, 1)

                for t in range(U + 1):
                    if t < U:
                        gated(t)
                    if t >= 1:
                        turned(t - 1)

        @block.scalar
        def _(act):
            for t in range(U):
                act.sem_inc(y_st[t], 16)
            act.sem_inc(rowsT_ps_ok, U)
            with act.Fori(0, SLOT_TILES // U) as it:
                def rows_copy(t):
                    act.wait_ge(rowsT_ps_ok, it * U + t + 1 + U)
                    nc.scalar.activation(rowsT[t % 2][:], rowsT_ps[:], ACT.Copy).then_inc(rowsT_ok, 1)

                def silu(t):
                    act.wait_ge(g_ok, it * U + t + 1)
                    nc.scalar.activation(gate[t % 2][:], g_ps[t % 2][:], ACT.Silu).then_inc(gate_ok, 1)

                def store(t):
                    act.wait_ge(y_ps_ok, it * U + t + 1)
                    act.wait_ge(y_st[t], (it + 1) * 16)
                    nc.scalar.activation(y[t][:], y_ps[t % 2][:], ACT.Copy).then_inc(y_ok, 1)
                    act.wait_ge(y_ok, it * U + t + 1)
                    act.dma_start(dram["y"][bass.ds((it * U + t) * P, P), :], y[t][:]).then_inc(y_st[t], 16)

                rows_copy(0)
                for t in range(U + 1):
                    if t < U:
                        silu(t)
                    if t + 1 < U:
                        rows_copy(t + 1)
                    if t >= 1:
                        store(t - 1)
            for t in range(U):
                act.wait_ge(y_st[t], 16 * (SLOT_TILES // U + 1))

        @block.tensor
        def _(pe):
            pe.wait_ge(ident_ok, 1)
            pe.wait_ge(ones_ok, 1)
            pe.wait_ge(w_in, 32 * EXPERTS)
            pe.wait_ge(bias_ok, 16 * 2 * PARTS)
            with pe.Fori(0, SLOT_TILES // U) as it:
                expert = [pe.value_load(tile_expert[0:1, bass.ds(it * U + t, 1)], min_val=0, max_val=EXPERTS - 1)
                          for t in range(U)]

                def rows_turned(t):
                    pe.wait_ge(rows_ok[t], (it + 1) * 16)
                    if t >= 1:
                        pe.wait_ge(rowsT_ok, it * U + t)
                    for c in range(DC):
                        last = nc.tensor.transpose(rowsT_ps[:, c * P:(c + 1) * P], rows[t][:, c * P:(c + 1) * P],
                                                   ident[:])
                    last.then_inc(rowsT_ps_ok, 1)

                def up(t):
                    pe.wait_ge(rowsT_ok, it * U + t + 1)
                    if t >= 2:
                        pe.wait_ge(hidden_ok, it * U + t - 1)
                    for out_ps, first, done in ((g_ps[t % 2], FF, g_ok), (a_ps[t % 2], 0, a_ok)):
                        nc.tensor.matmul(out_ps[:], ones[:], bias[0][:, bass.ds(expert[t], 1), first:first + FF].rearrange(
                            "p e n -> p (e n)"), start=True, stop=False)
                        for c in range(DC):
                            last = nc.tensor.matmul(out_ps[:], rowsT[t % 2][:, c * P:(c + 1) * P],
                                                    w1_sb[:, bass.ds(expert[t], 1), c, first:first + FF].rearrange(
                                                        "p e n -> p (e n)"), start=False, stop=(c == DC - 1))
                        last.then_inc(done, 1)

                def hidden_turned(t):
                    pe.wait_ge(hidden_ok, it * U + t + 1)
                    if t >= 1:
                        pe.wait_ge(hiddenT_ok, it * U + t)
                    for c in range(FC):
                        last = nc.tensor.transpose(hiddenT_ps[:, c * P:(c + 1) * P], hidden[t % 2][:, c * P:(c + 1) * P],
                                                   ident[:])
                    last.then_inc(hiddenT_ps_ok, 1)

                def down(t):
                    if t >= 2:
                        pe.wait_ge(y_ok, it * U + t - 1)
                    nc.tensor.matmul(y_ps[t % 2][:], ones[:], bias[1][:, bass.ds(expert[t], 1), :].rearrange(
                        "p e n -> p (e n)"), start=True, stop=False)
                    pe.wait_ge(hiddenT_ok, it * U + t + 1)
                    for c in range(FC):
                        last = nc.tensor.matmul(y_ps[t % 2][:], hiddenT[t % 2][:, c * P:(c + 1) * P],
                                                w2_sb[:, bass.ds(expert[t], 1), c, :].rearrange("p e n -> p (e n)"),
                                                start=False, stop=(c == FC - 1))
                    last.then_inc(y_ps_ok, 1)

                rows_turned(0)
                for t in range(U + 2):
                    if t + 1 < U:
                        rows_turned(t + 1)
                    if t < U:
                        up(t)
                    if 1 <= t <= U:
                        hidden_turned(t - 1)
                    if t >= 2:
                        down(t - 2)


def combine_phase(nc, dram, x2, weight, slot, out):
    RING = 4
    with ExitStack() as ctx:
        got = [ctx.enter_context(nc.sbuf_tensor(f"f_got{n}", [P, TOP, D], F32)) for n in range(RING)]
        part = [ctx.enter_context(nc.sbuf_tensor(f"f_part{n}", [P, D], F32)) for n in range(RING)]
        total = [ctx.enter_context(nc.sbuf_tensor(f"f_total{n}", [P, D], F32)) for n in range(RING)]
        got_ok = [ctx.enter_context(nc.semaphore(f"f_got_ok{n}")) for n in range(RING)]
        part_ok = ctx.enter_context(nc.semaphore("f_part_ok"))
        total_ok = ctx.enter_context(nc.semaphore("f_total_ok"))
        stored = [ctx.enter_context(nc.semaphore(f"f_stored{n}")) for n in range(RING)]
        block = ctx.enter_context(nc.Block())

        @block.gpsimd
        def _(pool):
            for t in range(NTILE):
                if t >= RING:
                    pool.wait_ge(total_ok, t - RING + 1)
                for k in range(TOP):
                    nc.gpsimd.indirect_dma_start(
                        out=got[t % RING][:, k, :], out_offset=None, in_=dram["y"],
                        in_offset=bass.IndirectOffsetOnAxis(ap=slot[:, k, t:t + 1], axis=0)).then_inc(
                            got_ok[t % RING], 16)

        @block.vector
        def _(dve):
            for t in range(NTILE):
                n = t % RING
                dve.wait_ge(got_ok[n], 16 * TOP * (t // RING + 1))
                nc.vector.scalar_tensor_tensor(out=part[n][:], in0=got[n][:, 0, :], scalar=weight[:, 0, t:t + 1],
                                               in1=x2[:, t, :], op0=ALU.mult, op1=ALU.add).then_inc(part_ok, 1)
                dve.wait_ge(part_ok, t + 1)
                if t >= RING:
                    dve.wait_ge(stored[n], 16 * (t // RING))
                nc.vector.scalar_tensor_tensor(out=total[n][:], in0=got[n][:, 1, :], scalar=weight[:, 1, t:t + 1],
                                               in1=part[n][:], op0=ALU.mult, op1=ALU.add).then_inc(total_ok, 1)

        @block.sync
        def _(sp):
            for t in range(NTILE):
                sp.wait_ge(total_ok, t + 1)
                sp.dma_start(out[t * P:(t + 1) * P, :], total[t % RING][:]).then_inc(stored[t % RING], 16)
            for n in range(RING):
                sp.wait_ge(stored[n], 16 * (NTILE // RING))


def clear_phase(nc, dram):
    TIMES = 8
    with nc.sbuf_tensor("z_zero", [P, SLOT_TILES // TIMES, D], F32) as zero, nc.semaphore("z_zeroed") as zeroed, \
            nc.semaphore("z_cleared") as cleared, nc.Block() as block:
        @block.vector
        def _(dve):
            nc.vector.memset(zero[:], 0.0).then_inc(zeroed, 1)

        @block.sync
        def _(sp):
            sp.wait_ge(zeroed, 1)
            for n, part in enumerate([dram["rows"].rearrange("(n p t) d -> n p t d", n=TIMES, p=P)[n]
                                      for n in range(TIMES)]):
                sp.dma_start(part, zero[:]).then_inc(cleared, 16)
            sp.wait_ge(cleared, 16 * TIMES)


def build(nc, x, w_dkv, w_uk, w_uv, w_uq, w_o, w_r, temp, w1, b1, w2, b2, out):
    dram = {
        "q_parts": nc.dram_tensor("q_parts", [DC, PARTS, P, NTOK], BF16).ap(),
        "k_parts": nc.dram_tensor("k_parts", [DC, PARTS, P, NTOK], BF16).ap(),
        "v": nc.dram_tensor("v_rows", [NTOK, D], F32).ap(),
        "ctx": nc.dram_tensor("ctx_cols", [NQUAD, P, SEQ], F32).ap(),
        "rows": nc.dram_tensor("slot_rows", [SLOT_TILES * P, D], F32).ap(),
        "y": nc.dram_tensor("slot_y", [SLOT_TILES * P, D], F32).ap(),
    }
    x = x.rearrange("b t d -> (b t) d")
    out = out.rearrange("b t d -> (b t) d")
    clear_phase(nc, dram)
    project_phase(nc, dram, x, w_dkv, w_uk, w_uv, w_uq)
    attention_phase(nc, dram)
    mixed_phase(nc, dram, x, w_o, w_r, temp, w1, b1, w2, b2, out)


_INS = ["L0_attn_x", "L0_attn_W_DKV", "L0_attn_W_UK", "L0_attn_W_UV", "L0_attn_W_UQ", "L0_attn_W_O", "L0_ffn_Wr",
        "L0_ffn_temp", "L0_ffn_W1", "L0_ffn_b1", "L0_ffn_W2", "L0_ffn_b2"]


def kernel(**inputs):
    import numpy as _np
    import concourse.bacc as _bacc
    from concourse.bass_utils import run_bass_kernel_spmd as _run

    nc = _bacc.Bacc("TRN2", target_bir_lowering=False, num_devices=1)
    arrays, args = {}, []
    for name in _INS:
        a = _np.ascontiguousarray(inputs[name])
        arrays[f"in_{name}"] = a
        args.append(nc.dram_tensor(f"in_{name}", a.shape, mybir.dt.from_np(a.dtype), kind="ExternalInput").ap())
    args.append(nc.dram_tensor("out_dram", (BATCH, SEQ, D), F32, kind="ExternalOutput").ap())
    build(nc, *args)
    r = _run(nc, [arrays], core_ids=[0])
    return r.results[0]["out_dram"]
```

```python
from contextlib import ExitStack

import concourse.bass as bass
from concourse import mybir

F32 = mybir.dt.float32
BF16 = mybir.dt.bfloat16
I32 = mybir.dt.int32
ALU = mybir.AluOpType
ACT = mybir.ActivationFunctionType
AX = mybir.AxisListType

P = 128
BATCH, SEQ, D = 4, 1024, 256
NTOK = BATCH * SEQ
DC = D // P
LAT = 64
HEADS, HD = 16, 16
QUAD = 4
NQUAD = BATCH * HEADS // QUAD
CHUNK = 512
NCHUNK = NTOK // CHUNK
TPC = CHUNK // P
QT = SEQ // P
EPS = 1e-5
SCALE = HD ** -0.5
EXPERTS, TOP, FF = 8, 2, 512
FC = FF // P
FC_EARLY = 3
PARTS = 3
RUNS = [(0, 0, 3), (3 * HD, 0, 2), (5 * HD, 0, 1)]
STACK = 6 * HD
MAXROWS = STACK + PARTS
MASKED = -3.0e38


def project_phase(nc, dram, x, w_dkv, w_uk, w_uv, w_uq):
    with ExitStack() as ctx:
        def sb(name, shape, dt=F32):
            return ctx.enter_context(nc.sbuf_tensor(name, shape, dt))

        def ps(name, shape, dt=F32):
            return ctx.enter_context(nc.psum_tensor(name, shape, dt))

        def sem(name):
            return ctx.enter_context(nc.semaphore(name))

        def pair(make, name, *rest):
            return [make(f"{name}{p}", *rest) for p in range(2)]

        ident = sb("a_ident", [P, P])
        wdkv = sb("a_wdkv", [P, DC, LAT])
        wuq = sb("a_wuq", [P, DC, D])
        wuk = sb("a_wuk", [LAT, D])
        wuq_rh = sb("a_wuq_rh", [P, DC, D])
        wuk_rh = sb("a_wuk_rh", [LAT, D])
        wuv = sb("a_wuv", [LAT, D])
        x_in = pair(sb, "a_x", [P, TPC, D])
        stats = sb("a_stats", [P, TPC, 6])
        mean_var = sb("a_mv", [P, TPC, 2])
        var_eps = sb("a_var_eps", [P, TPC])
        inv_var = sb("a_inv_var", [P, TPC])
        root = sb("a_root", [P, TPC])
        newton = sb("a_newton", [P, TPC])
        rstd = sb("a_rstd", [P, TPC])
        xn = pair(sb, "a_xn", [P, TPC, D])
        xnT = pair(sb, "a_xnT", [P, DC, CHUNK])
        ckvT = sb("a_ckvT", [LAT, CHUNK])
        part = [pair(sb, f"a_part_{qk}", [P, DC, PARTS, CHUNK], BF16) for qk in "qk"]
        rest = [pair(sb, f"a_rest_{qk}", [P, DC, CHUNK]) for qk in "qk"]
        v_out = pair(sb, "a_v", [P, TPC, D])

        tv_ps = ps("a_tv", [P, 2 * CHUNK])
        ckv_ps = ps("a_ckv", [P, CHUNK])
        qk_ps = [ps(f"a_{qk}_ps", [P, DC, CHUNK]) for qk in "qk"]

        w_in = sem("a_w_in")
        w_order_ok = sem("a_w_order_ok")
        ident0 = sem("a_ident0")
        ident_ok = sem("a_ident_ok")
        x_ok = pair(sem, "a_x_ok")
        stats_chain = sem("a_stats_chain")
        stats_turn = sem("a_stats_turn")
        root_chain = sem("a_root_chain")
        root_ok = sem("a_root_ok")
        inv_var_ok = sem("a_inv_var_ok")
        xn_ok = sem("a_xn_ok")
        xT_ps_ok = sem("a_xT_ps_ok")
        xnT_ok = sem("a_xnT_ok")
        ckv_ps_ok = sem("a_ckv_ps_ok")
        ckvT_ok = sem("a_ckvT_ok")
        v_ps_ok = sem("a_v_ps_ok")
        v_ok = sem("a_v_ok")
        v_st = pair(sem, "a_v_st")
        qk_ps_ok = [sem(f"a_{qk}_ps_ok") for qk in "qk"]
        part1_ok = [sem(f"a_part1_{qk}_ok") for qk in "qk"]
        rest_ok = [sem(f"a_rest_{qk}_ok") for qk in "qk"]
        part2_ok = [sem(f"a_part2_{qk}_ok") for qk in "qk"]
        part3_ok = [sem(f"a_part3_{qk}_ok") for qk in "qk"]
        part_out = [pair(sem, f"a_part_out_{qk}") for qk in "qk"]
        block = ctx.enter_context(nc.Block())

        def steps(eng, step):
            with eng.Fori(0, NCHUNK // 2 - 1) as it:
                for c in range(2):
                    step(it * 2 + c, c, NCHUNK)
            for c in range(2):
                step(NCHUNK - 2 + c, c, 1 - c)

        def rounds(n, c):
            return n // 2 if isinstance(n, int) else (n - c) // 2

        @block.sync
        def _(sp):
            def load(n, c):
                sp.dma_start(x_in[c][:], x[bass.ds(n * CHUNK, CHUNK), :].rearrange(
                    "(t p) d -> p t d", p=P)).then_inc(x_ok[c], 16)

            def step(n, c, left):
                if left >= 2:
                    sp.wait_ge(xn_ok, n + 1)
                    load(n + 2, c)
                for s, to in enumerate((dram["q_parts"], dram["k_parts"])):
                    sp.wait_ge(part3_ok[s], n + 1)
                    sp.dma_start(to[:, :, :, bass.ds(n * CHUNK, CHUNK)].rearrange("c g q n -> q c g n"),
                                 part[s][c][:]).then_inc(part_out[s][c], 16)
                sp.wait_ge(v_ok, n + 2)
                sp.dma_start(dram["v"][bass.ds(n * CHUNK, CHUNK), :].rearrange("(t p) d -> p t d", p=P),
                             v_out[c][:]).then_inc(v_st[c], 16)

            load(0, 0)
            sp.dma_start(wdkv[:], w_dkv.rearrange("(c p) n -> p c n", p=P)).then_inc(w_in, 16)
            sp.dma_start(wuq[:], w_uq.rearrange("(c p) n -> p c n", p=P)).then_inc(w_in, 16)
            load(1, 1)
            sp.dma_start(wuk[:], w_uk).then_inc(w_in, 16)
            sp.dma_start(wuv[:], w_uv).then_inc(w_in, 16)
            steps(sp, step)
            for p in range(2):
                for s in range(2):
                    sp.wait_ge(part_out[s][p], 16 * (NCHUNK // 2 + 1))
                sp.wait_ge(v_st[p], 16 * (NCHUNK // 2 + 1))

        @block.gpsimd
        def _(pool):
            nc.gpsimd.memset(ident[:], 0.0).then_inc(ident0, 1)
            pool.wait_ge(ident0, 1)
            nc.gpsimd.affine_select(out=ident[:], in_=ident[:], compare_op=ALU.not_equal, fill=1.0, base=0,
                                    pattern=[[-1, P]], channel_multiplier=1).then_inc(ident_ok, 1)
            pool.wait_ge(w_in, 64)
            for d in range(DC):
                for m in range(DC):
                    nc.gpsimd.tensor_copy(
                        wuq_rh[:, d, m * P:(m + 1) * P].rearrange("p (r h) -> p r h", r=HD),
                        wuq[:, d, m * P:(m + 1) * P].rearrange("p (h r) -> p r h", r=HD)).then_inc(w_order_ok, 1)
            for m in range(DC):
                nc.gpsimd.tensor_copy(wuk_rh[:, m * P:(m + 1) * P].rearrange("p (r h) -> p r h", r=HD),
                                      wuk[:, m * P:(m + 1) * P].rearrange("p (h r) -> p r h", r=HD)).then_inc(
                    w_order_ok, 1)

            def step(n, c, left):
                for s in range(2):
                    pool.wait_ge(part2_ok[s], n + 1)
                    nc.gpsimd.tensor_tensor(part[s][c][:, :, (2, 0)[s], :], rest[s][c][:], part[s][c][:, :, 1, :],
                                            ALU.subtract).then_inc(part3_ok[s], 1)

            steps(pool, step)

        @block.scalar
        def _(act):
            def take_root(n):
                act.wait_ge(inv_var_ok, n + 1)
                nc.scalar.activation(root[:], inv_var[:], ACT.Sqrt).then_inc(root_ok, 1)

            def turned(n, c):
                act.wait_ge(xT_ps_ok, n + 1)
                nc.scalar.activation(xnT[c][:].rearrange("p c n -> p (c n)"), tv_ps[:], ACT.Copy).then_inc(xnT_ok, 1)

            def first(n, c, s):
                act.wait_ge(qk_ps_ok[s], n + 1)
                act.wait_ge(part_out[s][c], (rounds(n, c) + 1) * 16)
                nc.scalar.activation(part[s][c][:, :, (0, 2)[s], :], qk_ps[s][:], ACT.Copy).then_inc(part1_ok[s], 1)

            def second(n, c, s):
                act.wait_ge(rest_ok[s], n + 2)
                nc.scalar.activation(part[s][c][:, :, 1, :], rest[s][c][:], ACT.Copy).then_inc(part2_ok[s], 1)

            def step(n, c, left):
                if left >= 1:
                    take_root(n + 1)
                first(n, c, 0)
                if left >= 1:
                    turned(n + 1, 1 - c)
                first(n, c, 1)
                second(n, c, 0)
                second(n, c, 1)

            take_root(0)
            turned(0, 0)
            steps(act, step)

        @block.vector
        def _(dve):
            def statistics(n, c):
                dve.wait_ge(x_ok[c], (rounds(n, c) + 1) * 16)
                dve.sem_inc(stats_turn, 1)
                for t in range(TPC):
                    last = nc.vector.bn_stats(stats[:, t, :], x_in[c][:, t, :])
                last.then_inc(stats_chain, 1)
                if not isinstance(n, int) or n >= 1:
                    dve.wait_ge(xn_ok, n)
                    dve.sem_inc(stats_turn, 1)
                dve.wait_ge(stats_chain, n * 3 + 1)
                dve.sem_inc(stats_turn, 1)
                for t in range(TPC):
                    last = nc.vector.bn_aggr(mean_var[:, t, :], stats[:, t, :])
                last.then_inc(stats_chain, 1)
                dve.wait_ge(stats_chain, n * 3 + 2)
                nc.vector.tensor_scalar(var_eps[:], mean_var[:, :, 1], EPS, None, ALU.add).then_inc(stats_chain, 1)
                dve.wait_ge(stats_chain, n * 3 + 3)
                nc.vector.reciprocal(inv_var[:], var_eps[:]).then_inc(inv_var_ok, 1)

            def normalise(n, c):
                dve.wait_ge(root_ok, n + 1)
                nc.vector.tensor_tensor(newton[:], root[:], root[:], ALU.mult).then_inc(root_chain, 1)
                dve.wait_ge(root_chain, n * 4 + 1)
                nc.vector.tensor_tensor(newton[:], newton[:], var_eps[:], ALU.mult).then_inc(root_chain, 1)
                dve.wait_ge(root_chain, n * 4 + 2)
                nc.vector.tensor_scalar(newton[:], newton[:], -0.5, 1.5, ALU.mult, ALU.add).then_inc(root_chain, 1)
                dve.wait_ge(root_chain, n * 4 + 3)
                nc.vector.tensor_tensor(rstd[:], root[:], newton[:], ALU.mult).then_inc(root_chain, 1)
                dve.wait_ge(root_chain, n * 4 + 4)
                for t in range(TPC):
                    last = nc.vector.tensor_scalar(xn[c][:, t, :], x_in[c][:, t, :], mean_var[:, t, 0:1],
                                                   rstd[:, t:t + 1], ALU.subtract, ALU.mult)
                last.then_inc(xn_ok, 1)

            def leave(n, c, s):
                dve.wait_ge(part1_ok[s], n + 1)
                nc.vector.tensor_tensor(rest[s][c][:], qk_ps[s][:], part[s][c][:, :, (0, 2)[s], :],
                                        ALU.subtract).then_inc(rest_ok[s], 1)

            def step(n, c, left):
                dve.wait_ge(ckv_ps_ok, n + 1)
                nc.vector.tensor_copy(ckvT[:], ckv_ps[0:LAT, :]).then_inc(ckvT_ok, 1)
                if left >= 1:
                    normalise(n + 1, 1 - c)
                leave(n, c, 0)
                leave(n, c, 1)
                dve.wait_ge(v_ps_ok, n + 1)
                dve.wait_ge(v_st[c], (rounds(n, c) + 1) * 16)
                nc.vector.tensor_copy(v_out[c][:].rearrange("p t d -> p (t d)"), tv_ps[:]).then_inc(v_ok, 1)
                if left >= 2:
                    statistics(n + 2, c)

            for p in range(2):
                for s in range(2):
                    dve.sem_inc(part_out[s][p], 16)
                dve.sem_inc(v_st[p], 16)
            for s in range(2):
                dve.sem_inc(rest_ok[s], 1)
            dve.sem_inc(v_ok, 1)
            statistics(0, 0)
            normalise(0, 0)
            statistics(1, 1)
            steps(dve, step)

        @block.tensor
        def _(pe):
            def turn(n, c):
                pe.wait_ge(xn_ok, n + 1)
                if not isinstance(n, int) or n >= 1:
                    pe.wait_ge(v_ok, n)
                for d in range(DC):
                    for t in range(TPC):
                        last = nc.tensor.transpose(tv_ps[:, d * CHUNK + t * P:d * CHUNK + (t + 1) * P],
                                                   xn[c][:, t, d * P:(d + 1) * P], ident[:])
                last.then_inc(xT_ps_ok, 1)

            def step(n, c, left):
                pe.wait_ge(xnT_ok, n + 1)
                for d in range(DC):
                    last = nc.tensor.matmul(ckv_ps[0:LAT, :], wdkv[:, d, :], xnT[c][:, d, :], start=(d == 0),
                                            stop=(d == DC - 1))
                last.then_inc(ckv_ps_ok, 1)
                pe.wait_ge(rest_ok[0], n + 1)
                for m in range(DC):
                    for d in range(DC):
                        last = nc.tensor.matmul(qk_ps[0][:, m, :], wuq_rh[:, d, m * P:(m + 1) * P], xnT[c][:, d, :],
                                                start=(d == 0), stop=(d == DC - 1))
                last.then_inc(qk_ps_ok[0], 1)
                if left >= 1:
                    turn(n + 1, 1 - c)
                pe.wait_ge(ckvT_ok, n + 1)
                pe.wait_ge(rest_ok[1], n + 1)
                for m in range(DC):
                    last = nc.tensor.matmul(qk_ps[1][:, m, :], wuk_rh[:, m * P:(m + 1) * P], ckvT[:],
                                            start=True, stop=True)
                last.then_inc(qk_ps_ok[1], 1)
                if left >= 1:
                    pe.wait_ge(xnT_ok, n + 2)
                for t in range(TPC):
                    last = nc.tensor.matmul(tv_ps[:, t * D:(t + 1) * D], ckvT[:, t * P:(t + 1) * P], wuv[:],
                                            start=True, stop=True)
                last.then_inc(v_ps_ok, 1)

            pe.wait_ge(ident_ok, 1)
            turn(0, 0)
            pe.wait_ge(w_in, 64)
            pe.wait_ge(w_order_ok, DC * DC + DC)
            steps(pe, step)


HALF = 512
PER_HALF = HALF // P
UNITS = QT + PER_HALF
PROB_BLOCKS = [(0, 0), (1, 0), (0, 1), (2, 0), (1, 1), (3, 0), (2, 1), (5, 1), (3, 1), (6, 1), (4, 1), (7, 1)]
MAX_BLOCKS = [(2, 0), (3, 0), (1, 0), (4, 0), (0, 0), (5, 0), (6, 1), (6, 0), (5, 1), (7, 0), (4, 1), (7, 1)]
HALF_DONE = [max(u for u, (_, half) in enumerate(PROB_BLOCKS) if half == h) + 1 for h in range(2)]


def prob_unit(u):
    j, half = PROB_BLOCKS[u]
    first = max(0, j * P - half * HALF)
    return j, half, first, HALF - first, j >= half * PER_HALF


def max_unit(u):
    i, half = MAX_BLOCKS[u]
    width = min(HALF, (i + 1) * P - half * HALF)
    return i, half, width, i < (half + 1) * PER_HALF


def block_at(k):
    return k // (2 * QUAD) * 2 + k % 2, k % (2 * QUAD) // 2


def index_of(unit, h):
    return unit // 2 * 2 * QUAD + 2 * h + unit % 2


def attention_phase(nc, dram, w1, w1_sb, w2, w2_early, loaded):
    RING = 4
    NM, NS = 3, 3
    NP = 16
    LEAD = UNITS + 4
    COMBINE_STEPS = 5
    TURN = 2
    TOTAL = NQUAD * UNITS
    LAG = 2
    PER_QUAD = UNITS * QUAD
    HT = QUAD * QT
    DIAGONALS = QUAD * QT

    def turned_at(unit):
        g, u = divmod(unit - TURN, UNITS)
        return g - 1 if u == 0 and 1 <= g <= NQUAD else None

    max_items = []
    for unit in range(TOTAL + TURN + 1):
        if turned_at(unit) is not None:
            max_items.append(("turn", turned_at(unit)))
        if unit < TOTAL:
            max_items += [("score", unit * QUAD + h) for h in range(QUAD)]
    place = {item: k for k, item in enumerate(max_items)}
    with ExitStack() as ctx:
        def sb(name, shape, dt=F32):
            return ctx.enter_context(nc.sbuf_tensor(name, shape, dt))

        def ps(name, shape, dt=F32):
            return ctx.enter_context(nc.psum_tensor(name, shape, dt))

        def sem(name):
            return ctx.enter_context(nc.semaphore(name))

        def several(make, n, name, *rest):
            return [make(f"{name}{p}", *rest) for p in range(n)]

        ident = sb("b_ident", [P, P], BF16)
        mask_max = sb("b_mask_max", [P, HALF])
        q_st = several(sb, RING, "b_q_st", [P, QUAD, SEQ], BF16)
        k_st = several(sb, RING, "b_k_st", [P, QUAD, SEQ], BF16)
        v_in = several(sb, 2, "b_v_in", [P, QT, QUAD * HD])
        v_aug = several(sb, 2, "b_v_aug", [P, QT, QUAD, HD, 2])
        prob = several(sb, NP, "b_prob", [P, HALF])
        neg_max = several(sb, 2, "b_neg_max", [P, 2, QUAD, QT])
        max_part = sb("b_max_part", [P, PARTS, HT], BF16)
        max_rest = sb("b_max_rest", [P, HT])
        max_rows = several(sb, 2, "b_max_rows", [PARTS * HT, P], BF16)
        ctx_out = several(sb, 2, "b_ctx_out", [P, SEQ])

        max_ps = several(ps, NM, "b_max_ps", [P, HALF])
        prob_ps = several(ps, NS, "b_prob_ps", [P, HALF])
        acc_ps = several(ps, 2, "b_acc_ps", [P, HALF])

        const0 = sem("b_const0")
        const_ok = sem("b_const_ok")
        ones_ok = sem("b_ones_ok")
        stack_ok = several(sem, RING, "b_stack_ok")
        v_in_ok = several(sem, 2, "b_v_in_ok")
        v_aug_ok = sem("b_v_aug_ok")
        max_sc_ok = sem("b_max_sc_ok")
        max_done = sem("b_max_done")
        chain = sem("b_chain")
        max_part_ok = sem("b_max_part_ok")
        rows_ps_ok = sem("b_rows_ps_ok")
        rows_ok = sem("b_rows_ok")
        rows_in = several(sem, RING, "b_rows_in")
        prob_sc_ok = sem("b_prob_sc_ok")
        prob_ok = sem("b_prob_ok")
        causal_ok = sem("b_causal_ok")
        pv_ok = sem("b_pv_ok")
        acc_out = several(sem, 2, "b_acc_out")
        ctx_st = several(sem, 2, "b_ctx_st")
        block = ctx.enter_context(nc.Block())
        LOADS = 2 * len(RUNS)

        def turned_ps(g):
            return max_ps[place["turn", g] % NM][0:PARTS * HT, 0:P // 2].bitcast(BF16)

        @block.sync
        def _(sp):
            def load(g):
                b, w = divmod(g, RING)
                if g >= RING:
                    sp.wait_ge(prob_sc_ok, PER_QUAD * (g - RING + 1))
                c, first = divmod(w * QUAD, P // HD)
                for stack, parts, reverse in ((q_st[w], dram["q_parts"], False), (k_st[w], dram["k_parts"], True)):
                    rows = parts[c].rearrange("g (r h) n -> (g r) h n", r=HD)
                    for to, part, n in RUNS:
                        start = (PARTS - n if reverse else part) * HD
                        sp.dma_start(stack[to:to + n * HD, :, :],
                                     rows[start:start + n * HD, first:first + QUAD, b * SEQ:(b + 1) * SEQ]).then_inc(
                            stack_ok[w], 16)
                if g >= 2:
                    sp.wait_ge(v_aug_ok, g - 1)
                sp.dma_start(v_in[g % 2][:], dram["v"].rearrange("(b t p) d -> b p t d", b=BATCH, p=P)[
                    b, :, :, w * QUAD * HD:(w + 1) * QUAD * HD]).then_inc(v_in_ok[g % 2], 16)

            def store(g):
                sp.wait_ge(acc_out[1], g + 1)
                sp.dma_start(dram["ctx"][g], ctx_out[g % 2][:]).then_inc(ctx_st[g % 2], 16)
                sp.dma_start(dram["den"][g * QUAD:(g + 1) * QUAD, :],
                             ctx_out[g % 2][1:P:2 * HD, :]).then_inc(ctx_st[g % 2], 16)

            load(0)
            for g in range(NQUAD + 2):
                if g + 1 < NQUAD:
                    load(g + 1)
                if g < EXPERTS:
                    sp.dma_start(w1_sb[:, g, :, :], w1[g].rearrange("(c p) n -> p c n", p=P)).then_inc(loaded, 16)
                elif g < EXPERTS + FC_EARLY:
                    f = g - EXPERTS
                    sp.dma_start(w2_early[f][:], w2.rearrange("e (f p) n -> f p e n", p=P)[f]).then_inc(loaded, 16)
                if 0 <= g - 1 < NQUAD:
                    w = (g - 1) % RING
                    sp.wait_ge(rows_ok, g)
                    for n in range(PARTS):
                        sp.dma_start(q_st[w][STACK + n:STACK + n + 1, :, :].rearrange("o h (t n) -> o (h t) n", n=P),
                                     max_rows[(g - 1) % 2][n * HT:(n + 1) * HT, :]).then_inc(rows_in[w], 16)
                if g >= 2:
                    store(g - 2)
            for p in range(2):
                sp.wait_ge(ctx_st[p], 32 * (NQUAD // 2))

        @block.gpsimd
        def _(pool):
            for n, tile in enumerate((ident, mask_max)):
                nc.gpsimd.memset(tile[:], 0.0).then_inc(const0, 1)
            pool.wait_ge(const0, 2)
            nc.gpsimd.affine_select(out=ident[:], in_=ident[:], compare_op=ALU.not_equal, fill=1.0, base=0,
                                    pattern=[[-1, P]], channel_multiplier=1).then_inc(const_ok, 1)
            nc.gpsimd.affine_select(out=mask_max[:], in_=mask_max[:], compare_op=ALU.is_ge, fill=MASKED,
                                    base=HALF - P, pattern=[[-1, HALF]], channel_multiplier=1).then_inc(const_ok, 1)
            for n, tile in enumerate(v_aug + k_st):
                nc.gpsimd.memset(tile[:] if n < 2 else tile[STACK:P, :, :], 1.0).then_inc(ones_ok, 1)
                pool.wait_ge(ones_ok, n + 1)

            def v_copy(g):
                pool.wait_ge(v_in_ok[g % 2], 16 * (g // 2 + 1))
                if g >= 2:
                    pool.wait_ge(pv_ok, UNITS * (g - 1))
                nc.gpsimd.tensor_copy(v_aug[g % 2][:, :, :, :, 0], v_in[g % 2][:].rearrange(
                    "p t (h r) -> p t h r", h=QUAD)).then_inc(v_aug_ok, 1)

            v_copy(0)
            for unit in range(TOTAL):
                g, u = divmod(unit, UNITS)
                if u == PER_HALF and g + 1 < NQUAD:
                    v_copy(g + 1)
                for n in range(unit * QUAD, (unit + 1) * QUAD):
                    if prob_unit(block_at(n)[0] % UNITS)[4]:
                        pool.wait_ge(prob_ok, n + 1)
                        nc.gpsimd.affine_select(out=prob[n % NP][:, 0:P], in_=prob[n % NP][:, 0:P],
                                                compare_op=ALU.is_ge, fill=0.0, base=0, pattern=[[1, P]],
                                                channel_multiplier=-1).then_inc(causal_ok, 1)

        @block.vector
        def _(dve):
            def combine(g, step):
                halves = neg_max[g % 2]
                both = halves[:, 0, :, PER_HALF:QT]
                whole = halves[:, 0, :, :].rearrange("p h t -> p (h t)")
                if step == 0:
                    dve.wait_ge(max_done, (g + 1) * PER_QUAD)
                    nc.vector.tensor_tensor(both, both, halves[:, 1, :, PER_HALF:QT], ALU.min).then_inc(chain, 1)
                elif step == 1:
                    if g >= 1:
                        dve.wait_ge(rows_ps_ok, g)
                    dve.wait_ge(chain, 4 * g + 1)
                    nc.vector.tensor_copy(max_part[:, 0, :], whole).then_inc(chain, 1)
                elif step == 2:
                    dve.wait_ge(chain, 4 * g + 2)
                    nc.vector.tensor_tensor(max_rest[:], whole, max_part[:, 0, :], ALU.subtract).then_inc(chain, 1)
                elif step == 3:
                    dve.wait_ge(chain, 4 * g + 3)
                    nc.vector.tensor_copy(max_part[:, 1, :], max_rest[:]).then_inc(chain, 1)
                elif step == 4:
                    dve.wait_ge(chain, 4 * g + 4)
                    nc.vector.tensor_tensor(max_part[:, 2, :], max_rest[:], max_part[:, 1, :],
                                            ALU.subtract).then_inc(max_part_ok, 1)

            for unit in range(TOTAL):
                g = unit // UNITS
                for n in range(unit * QUAD, (unit + 1) * QUAD):
                    block, h = block_at(n)
                    i, half, width, diagonal = max_unit(block % UNITS)
                    dve.wait_ge(max_sc_ok, n + 1)
                    scores = max_ps[place["score", n] % NM][:, 0:width]
                    to = neg_max[g % 2][:, half, h, i:i + 1]
                    if diagonal:
                        nc.vector.tensor_tensor_reduce(scores, scores, mask_max[:, HALF - width:HALF],
                                                       -1.0, -MASKED, ALU.add, ALU.min, to).then_inc(max_done, 1)
                    else:
                        nc.vector.tensor_reduce(to, scores, AX.X, ALU.max, negate=True).then_inc(max_done, 1)
                    if g >= 1 and n - g * PER_QUAD < COMBINE_STEPS:
                        combine(g - 1, n - g * PER_QUAD)
            for step in range(COMBINE_STEPS):
                combine(NQUAD - 1, step)

        @block.scalar
        def _(act):
            def acc_copy(g, half):
                act.wait_ge(pv_ok, g * UNITS + HALF_DONE[half])
                if g >= 2 and half == 0:
                    act.wait_ge(ctx_st[g % 2], 32 * (g // 2))
                nc.scalar.activation(ctx_out[g % 2][:, half * HALF:(half + 1) * HALF], acc_ps[half][:],
                                     ACT.Copy).then_inc(acc_out[half], 1)

            def rows_copy(g):
                act.wait_ge(rows_ps_ok, g + 1)
                if g >= 2:
                    act.wait_ge(rows_in[(g - 2) % RING], 16 * PARTS * ((g - 2) // RING + 1))
                nc.scalar.activation(max_rows[g % 2][:], turned_ps(g), ACT.Copy).then_inc(rows_ok, 1)

            for unit in range(-LEAD, TOTAL):
                if turned_at(unit + LEAD) is not None:
                    rows_copy(turned_at(unit + LEAD))
                if unit < 0:
                    continue
                g, u = divmod(unit, UNITS)
                if u == LAG and g >= 1:
                    acc_copy(g - 1, 1)
                if u == HALF_DONE[0] + LAG:
                    acc_copy(g, 0)
                for n in range(unit * QUAD, (unit + 1) * QUAD):
                    width = prob_unit(block_at(n)[0] % UNITS)[3]
                    act.wait_ge(prob_sc_ok, n + 1)
                    if n >= NP:
                        act.wait_ge(pv_ok, block_at(n - NP)[0] + 1)
                    nc.scalar.activation(prob[n % NP][:, 0:width], prob_ps[n % NS][:, 0:width], ACT.Exp,
                                         scale=SCALE).then_inc(prob_ok, 1)
            acc_copy(NQUAD - 1, 1)

        @block.tensor
        def _(pe):
            def bank_free(item):
                if place[item] < NM:
                    return
                kind, n = max_items[place[item] - NM]
                if kind == "score":
                    pe.wait_ge(max_done, n + 1)
                else:
                    pe.wait_ge(rows_ok, n + 1)

            def max_scores(n):
                unit, h = block_at(n)
                g, u = divmod(unit, UNITS)
                i, half, width, _ = max_unit(u)
                item = ("score", n)
                if u == 0 and h == 0:
                    pe.wait_ge(stack_ok[g % RING], 16 * LOADS * (g // RING + 1))
                bank_free(item)
                out = max_ps[place[item] % NM]
                nc.tensor.matmul(out[:, 0:width], q_st[g % RING][0:STACK, h, i * P:(i + 1) * P],
                                 k_st[g % RING][0:STACK, h, half * HALF:half * HALF + width],
                                 start=True, stop=True).then_inc(max_sc_ok, 1)

            def prob_scores(n):
                unit, h = block_at(n)
                g, u = divmod(unit, UNITS)
                j, half, first, width, _ = prob_unit(u)
                if unit == 0 and h == 0:
                    pe.wait_ge(ones_ok, RING + 2)
                if u == 0 and h == 0:
                    pe.wait_ge(rows_in[g % RING], 16 * PARTS * (g // RING + 1))
                if n >= NS:
                    pe.wait_ge(prob_ok, n - NS + 1)
                q0 = half * HALF + first
                nc.tensor.matmul(prob_ps[n % NS][:, 0:width], k_st[g % RING][0:MAXROWS, h, j * P:(j + 1) * P],
                                 q_st[g % RING][0:MAXROWS, h, q0:q0 + width], start=True,
                                 stop=True).then_inc(prob_sc_ok, 1)

            def products(unit):
                g, u = divmod(unit, UNITS)
                j, half, first, width, diagonal = prob_unit(u)
                if u == 0:
                    pe.wait_ge(v_aug_ok, g + 1)
                if j == 0 and g >= 1:
                    pe.wait_ge(acc_out[half], g)
                if diagonal:
                    cut = sum(prob_unit(block_at(n)[0])[4] for n in range(index_of(u, QUAD - 1) + 1))
                    pe.wait_ge(causal_ok, g * DIAGONALS + cut)
                else:
                    pe.wait_ge(prob_ok, index_of(unit, QUAD - 1) + 1)
                for h in range(QUAD):
                    mm = nc.tensor.matmul(acc_ps[half][32 * h:32 * h + 2 * HD, first:first + width],
                                          v_aug[g % 2][:, j, h, :, :].rearrange("p r s -> p (r s)"),
                                          prob[index_of(unit, h) % NP][:, 0:width],
                                          start=(j == 0), stop=(j == (PER_HALF if half == 0 else QT) - 1),
                                          tile_position=(0, 32 * h))
                mm.then_inc(pv_ok, 1)

            def max_rows_transposed(g):
                pe.wait_ge(max_part_ok, g + 1)
                bank_free(("turn", g))
                nc.tensor.transpose(turned_ps(g), max_part[:].rearrange("p a n -> p (a n)"), ident[:]).then_inc(
                    rows_ps_ok, 1)

            pe.wait_ge(const_ok, 2)
            for unit in range(TOTAL + LEAD + LAG):
                if turned_at(unit) is not None:
                    max_rows_transposed(turned_at(unit))
                for n in range(unit * QUAD, (unit + 1) * QUAD):
                    if unit < TOTAL:
                        max_scores(n)
                    if 0 <= unit - LEAD < TOTAL:
                        prob_scores(n - LEAD * QUAD)
                if unit - LEAD - LAG >= 0:
                    products(unit - LEAD - LAG)


BT = SEQ // P
REGION = NTOK + P
ROW_W, ROW_ID, ROW = D, D + 1, D + 2
SLOT_TILES = (TOP * NTOK + EXPERTS * (P - 1)) // P
ROW_BUFS = 5
SLOT_UNROLL = 2 * ROW_BUFS
SLOT_LEAD = 2 + (SLOT_TILES - 2) % SLOT_UNROLL
SPARE = SLOT_TILES + 1 - TOP * NTOK // P
OUT_ROWS = NTOK + P


def mixed_phase(nc, dram, x, w_o, w_r, temp, b_dram, w2, w1_sb, w2_early, loaded, out):
    with ExitStack() as ctx:
        def sb(name, shape, dt=F32):
            return ctx.enter_context(nc.sbuf_tensor(name, shape, dt))

        tile_expert = sb("m_tile_expert", [1, SLOT_TILES + 1], I32)
        tile_row = sb("m_tile_row", [1, SLOT_TILES + 1], I32)
        ident = sb("m_ident", [P, P])
        bias = [sb("m_b1", [P, EXPERTS, 2 * FF]), sb("m_b2", [P, EXPERTS, D])]
        w2_sb = w2_early + [sb(f"m_w2_{f}", [P, EXPERTS, D]) for f in range(FC_EARLY, FC)]
        weights = (w1_sb, w2_sb, bias, loaded)
        route_phase(nc, dram, x, w_o, w_r, temp, b_dram, w2, weights, ident, tile_expert, tile_row, out)
        expert_phase(nc, dram, weights, ident, tile_expert, tile_row, out)


def route_phase(nc, dram, x, w_o, w_r, temp, b_dram, w2, weights, ident, tile_expert, tile_row, out):
    _, w2_sb, bias, loaded = weights
    BIG = 3.0e38
    PAIRS = BT // 2
    SPREADS = DC * SEQ // CHUNK
    with ExitStack() as ctx:
        def sb(name, shape, dt=F32):
            return ctx.enter_context(nc.sbuf_tensor(name, shape, dt))

        def ps(name, shape, dt=F32):
            return ctx.enter_context(nc.psum_tensor(name, shape, dt))

        def sem(name):
            return ctx.enter_context(nc.semaphore(name))

        def pair(make, name, *rest):
            return [make(f"{name}{p}", *rest) for p in range(2)]

        wo = sb("c_wo", [P, DC, D])
        wr = sb("c_wr", [P, DC, EXPERTS])
        temp_in = sb("c_temp", [P, 1])
        inv_temp = sb("c_inv_temp", [P, 1])
        spread = sb("c_spread", [P, DC, BT, P])
        den_in = sb("c_den_in", [P, P])
        inv_den = sb("c_inv_den", [P, P])
        heads = sb("c_heads", [P, DC, SEQ])
        x_in = sb("c_x_in", [P, BT, D])
        x2 = sb("c_x2", [P, BT, D])
        stats = sb("c_stats", [P, BT, 6])
        mean_var = sb("c_mv", [P, BT, 2])
        var_eps = sb("c_var_eps", [P, BT])
        inv_var = sb("c_inv_var", [P, BT])
        root = sb("c_root", [P, BT])
        newton = sb("c_newton", [P, BT])
        rstd = sb("c_rstd", [P, BT])
        first_row = pair(sb, "c_first_row", [P, BT, ROW])
        second_row = sb("c_second_row", [P, BT, ROW])
        xnT = pair(sb, "c_xnT", [P, 2, DC, P])

        tokens = [P, BT, EXPERTS]
        order = sb("r_order", tokens)
        logits = sb("r_logits", tokens)
        rank = sb("r_rank", tokens)
        second = sb("r_second", tokens)
        one_hot = pair(sb, "r_one_hot", tokens)
        picked = sb("r_picked", tokens)
        top = pair(sb, "r_top", [P, BT])
        key = sb("r_key", [P, BT])
        gap = sb("r_gap", [P, BT])
        power = sb("r_power", [P, BT])
        total = sb("r_total", [P, BT])
        slot_f = sb("r_slot_f", [P, BT])
        slot = pair(sb, "r_slot", [P, TOP, BT], I32)
        token_f = sb("r_token_f", [P, BT])
        token_id = pair(sb, "r_token_id", [P, BT], I32)
        second_weight = pair(sb, "r_second_weight", [P, BT])
        chosen = sb("r_chosen", [P, EXPERTS, BT], BF16)
        before = sb("r_before", [P, P], BF16)
        ones = sb("r_ones", [P, P], BF16)
        ones_row = sb("r_ones_row", [P, EXPERTS * BT])
        running = sb("r_running", [P, EXPERTS, BT])
        place = sb("r_place", [P, EXPERTS, BT])
        count = sb("r_count", [P, EXPERTS])
        start = sb("r_start", [P, EXPERTS])
        base = sb("r_base", [P, EXPERTS])
        region = sb("r_region", [P, EXPERTS])
        pad_row = sb("r_pad_row", [P, ROW])
        pad_slot_f = sb("r_pad_slot_f", [P, EXPERTS])
        pad_slot = sb("r_pad_slot", [1, EXPERTS], I32)
        filled = sb("r_filled", [P, EXPERTS])
        tiles = sb("r_tiles", [P, EXPERTS])
        tiles_end = sb("r_tiles_end", [P, EXPERTS])
        jump = sb("r_jump", [P, EXPERTS])
        tile_index = sb("r_tile_index", [P, SLOT_TILES + 1])
        passed = x_in[:].rearrange("p t d -> p (t d)")[:, 0:(SLOT_TILES + 1) * EXPERTS].rearrange(
            "p (n e) -> p n e", e=EXPERTS)
        tile_f = sb("r_tile_f", [P, SLOT_TILES + 1])

        spread_ps = pair(ps, "c_spread_ps", [P, CHUNK])
        proj_ps = [ps(f"c_proj_ps{n}", [P, 2, D]) for n in range(PAIRS)]
        xnT_ps = ps("c_xnT_ps", [P, 2 * D])
        router_ps = ps("c_router_ps", [P, 3, EXPERTS * BT])
        logit_ps = router_ps[:, 0, :].rearrange("p (t e) -> p t e", t=BT)
        prefix_ps = router_ps[:, 1, :].rearrange("p (e t) -> p e t", t=BT)
        total_ps = router_ps[:, 2, :].rearrange("p (e t) -> p e t", t=BT)

        small_in = sem("c_small_in")
        zeroed = sem("c_zeroed")
        const_ok = sem("c_const_ok")
        den_in_ok = sem("c_den_in_ok")
        ctx_in_ok = sem("c_ctx_in_ok")
        x_in_ok = sem("c_x_in_ok")
        inv_den_ok = sem("c_inv_den_ok")
        spread_ps_ok = sem("c_spread_ps_ok")
        heads_ok = sem("c_heads_ok")
        proj_ok = sem("c_proj_ok")
        x2_ok = sem("c_x2_ok")
        x2_st = sem("c_x2_st")
        step = sem("c_step")
        inv_var_ok = sem("c_inv_var_ok")
        root_ok = sem("c_root_ok")
        xn_ok = sem("c_xn_ok")
        copy_ok = sem("c_copy_ok")
        xnT_ps_ok = sem("c_xnT_ps_ok")
        xnT_ok = sem("c_xnT_ok")
        logit_ps_ok = sem("c_logit_ps_ok")
        gap_ok = sem("r_gap_ok")
        power_ok = sem("r_power_ok")
        chosen_ok = sem("r_chosen_ok")
        counts_ok = sem("r_counts_ok")
        slot_ok = sem("r_slot_ok")
        first_in_slot = pair(sem, "r_first_in_slot")
        second_in_slot = sem("r_second_in_slot")
        second_ok = sem("r_second_ok")
        pad_row_ok = sem("r_pad_row_ok")
        pad_slot_ok = sem("r_pad_slot_ok")
        spare_st = sem("r_spare_st")
        block = ctx.enter_context(nc.Block())

        @block.sync
        def _(sp):
            def load(b):
                if b:
                    sp.wait_ge(inv_den_ok, b)
                sp.dma_start(den_in[:], dram["den"][b * HEADS:(b + 1) * HEADS, :].rearrange(
                    "h (t n) -> (h t) n", n=P)).then_inc(den_in_ok, 16)
                if b:
                    sp.wait_ge(proj_ok, b * PAIRS)
                context = dram["ctx"].rearrange("g (q s) n -> s (g q) n", s=2)[0]
                sp.dma_start(heads[:], context[b * D:(b + 1) * D, :].rearrange("(c p) n -> p c n", p=P)).then_inc(
                    ctx_in_ok, 16)
                if b:
                    sp.wait_ge(x2_ok, b * PAIRS)
                if b == 0:
                    sp.dma_start(wo[:], w_o.rearrange("(c p) n -> p c n", p=P)).then_inc(small_in, 16)
                    sp.dma_start(wr[:], w_r.rearrange("(c p) n -> p c n", p=P)).then_inc(small_in, 16)
                    sp.dma_start(temp_in[:], temp.rearrange("(o n) -> o n", o=1).to_broadcast([P, 1])).then_inc(
                        small_in, 16)
                sp.dma_start(x_in[:], x[b * SEQ:(b + 1) * SEQ, :].rearrange("(t p) d -> p t d", p=P)).then_inc(
                    x_in_ok, 16)

            load(0)
            for b in range(BATCH):
                if b + 1 < BATCH:
                    load(b + 1)
                for f in range(FC_EARLY, FC) if b == 0 else ():
                    sp.dma_start(w2_sb[f][:], w2.rearrange("e (f p) n -> f p e n", p=P)[f]).then_inc(loaded, 16)
                for e in range(b * EXPERTS // BATCH, (b + 1) * EXPERTS // BATCH):
                    for n in range(2):
                        sp.dma_start(bias[n][:, e, :], b_dram[n][e:e + 1, :].to_broadcast(
                            [P, b_dram[n].shape[1]])).then_inc(loaded, 16)
                sp.wait_ge(x2_ok, (b + 1) * PAIRS)
                sp.dma_start(out[b * SEQ:(b + 1) * SEQ, :].rearrange("(t p) d -> p t d", p=P),
                             x2[:]).then_inc(x2_st, 16)
            sp.wait_ge(pad_row_ok, 1)
            sp.dma_start(out[NTOK:OUT_ROWS, :], pad_row[:, 0:D]).then_inc(spare_st, 16)
            for n in range(SPARE):
                first = EXPERTS * REGION + n * P
                sp.dma_start(dram["rows"][first:first + P, :], pad_row[:]).then_inc(spare_st, 16)
            sp.wait_ge(pad_slot_ok, 1)
            for e in range(EXPERTS):
                first = sp.value_load(pad_slot[0:1, e:e + 1], min_val=0, max_val=EXPERTS * REGION - P)
                sp.dma_start(dram["rows"][bass.ds(first, P), :], pad_row[:]).then_inc(spare_st, 16)
            sp.wait_ge(spare_st, 16 * (1 + SPARE + EXPERTS))
            sp.wait_ge(x2_st, 16 * BATCH)

        @block.gpsimd
        def _(pool):
            nc.gpsimd.memset(spread[:], 0.0).then_inc(zeroed, 1)
            pool.wait_ge(zeroed, 1)
            per_chunk = P // HD
            nc.gpsimd.affine_select(out=spread[:].rearrange("p c t (h r) -> p c t h r", r=HD),
                                    in_=spread[:].rearrange("p c t (h r) -> p c t h r", r=HD),
                                    compare_op=ALU.not_equal, fill=1.0, base=0,
                                    pattern=[[-BT * per_chunk, DC], [-1, BT], [-BT, per_chunk], [0, HD]],
                                    channel_multiplier=1).then_inc(const_ok, 1)
            nc.gpsimd.memset(ident[:], 0.0).then_inc(zeroed, 1)
            nc.gpsimd.memset(before[:], 1.0).then_inc(zeroed, 1)
            nc.gpsimd.memset(pad_row[:], 0.0).then_inc(zeroed, 1)
            pool.wait_ge(zeroed, 4)
            nc.gpsimd.affine_select(out=ident[:], in_=ident[:], compare_op=ALU.not_equal, fill=1.0, base=0,
                                    pattern=[[-1, P]], channel_multiplier=1).then_inc(const_ok, 1)
            nc.gpsimd.affine_select(out=before[:], in_=before[:], compare_op=ALU.is_gt, fill=0.0, base=0,
                                    pattern=[[1, P]], channel_multiplier=-1).then_inc(const_ok, 1)
            for tile, pattern, base0, by in ((order, [[0, BT], [-1, EXPERTS]], EXPERTS, 0),
                                             (token_f, [[P, BT]], 0, 1),
                                             (tile_index, [[1, SLOT_TILES + 1]], 0, 0),
                                             (region, [[REGION, EXPERTS]], 0, 0)):
                nc.gpsimd.iota(tile[:], pattern, base=base0, channel_multiplier=by,
                               allow_small_or_imprecise_dtypes=True).then_inc(const_ok, 1)
            nc.gpsimd.iota(pad_row[:, ROW_ID:ROW].bitcast(I32), [[0, 1]], base=NTOK,
                           channel_multiplier=1).then_inc(pad_row_ok, 1)
            def scatter(b, k, row, done):
                pool.wait_ge(slot_ok, TOP * b + k + 1)
                for t in range(BT):
                    to = bass.IndirectOffsetOnAxis(ap=slot[b % 2][:, k, t:t + 1], axis=0)
                    nc.gpsimd.indirect_dma_start(out=dram["rows"], out_offset=to, in_=row[:, t, :],
                                                 in_offset=None).then_inc(done, 16)

            for b in range(BATCH):
                scatter(b, 0, first_row[b % 2], first_in_slot[b % 2])
                if b:
                    pool.wait_ge(second_in_slot, 16 * BT * b)
                nc.gpsimd.tensor_copy(second_row[:, :, ROW_W], second_weight[b % 2][:]).then_inc(second_ok, 1)
                nc.gpsimd.tensor_copy(second_row[:, :, ROW_ID].bitcast(I32), token_id[b % 2][:]).then_inc(second_ok, 1)
                pool.wait_ge(second_ok, 2 * (b + 1))
                pool.wait_ge(copy_ok, b + 1)
                scatter(b, 1, second_row, second_in_slot)
            for p in range(2):
                pool.wait_ge(first_in_slot[p], 16 * BT * BATCH // 2)
            pool.wait_ge(second_in_slot, 16 * BT * BATCH)

        @block.vector
        def _(dve):
            done = [0]

            def then(ins):
                done[0] += 1
                ins.then_inc(step, 1)
                dve.wait_ge(step, done[0])

            def wide(ap, n=EXPERTS):
                return ap.unsqueeze(2).to_broadcast([P, ap.shape[1], n])

            def invert(b):
                dve.wait_ge(den_in_ok, 16 * (b + 1))
                if b:
                    dve.wait_ge(spread_ps_ok, b * SPREADS)
                nc.vector.reciprocal(inv_den[:], den_in[:]).then_inc(inv_den_ok, 1)

            def normalise(b):
                dve.wait_ge(ctx_in_ok, 16 * (b + 1))
                for k in range(SPREADS):
                    n = b * SPREADS + k
                    half = heads[:, k % DC, k // DC * CHUNK:(k // DC + 1) * CHUNK]
                    dve.wait_ge(spread_ps_ok, n + 1)
                    nc.vector.tensor_tensor(half, half, spread_ps[n % 2][:], ALU.mult).then_inc(heads_ok, 1)

            def residual(b):
                dve.wait_ge(x_in_ok, 16 * (b + 1))
                if b:
                    dve.wait_ge(xn_ok, PAIRS * b)
                    dve.wait_ge(x2_st, 16 * b)
                for t in range(PAIRS):
                    n = b * PAIRS + t
                    dve.wait_ge(proj_ok, n + 1)
                    nc.vector.tensor_tensor(x2[:, 2 * t:2 * t + 2, :], proj_ps[t][:], x_in[:, 2 * t:2 * t + 2, :],
                                            ALU.add).then_inc(x2_ok, 1)

            def statistics(b):
                for t in range(BT):
                    if t % 2 == 0:
                        dve.wait_ge(x2_ok, b * PAIRS + t // 2 + 1)
                    last = nc.vector.bn_stats(stats[:, t, :], x2[:, t, :])
                then(last)
                for t in range(BT):
                    last = nc.vector.bn_aggr(mean_var[:, t, :], stats[:, t, :])
                then(last)
                then(nc.vector.tensor_scalar(var_eps[:], mean_var[:, :, 1], EPS, None, ALU.add))
                nc.vector.reciprocal(inv_var[:], var_eps[:]).then_inc(inv_var_ok, 1)

            def layer_norm(b):
                dve.wait_ge(root_ok, b + 1)
                then(nc.vector.tensor_tensor(newton[:], root[:], root[:], ALU.mult))
                then(nc.vector.tensor_tensor(newton[:], newton[:], var_eps[:], ALU.mult))
                then(nc.vector.tensor_scalar(newton[:], newton[:], -0.5, 1.5, ALU.mult, ALU.add))
                then(nc.vector.tensor_tensor(rstd[:], root[:], newton[:], ALU.mult))
                if b >= 2:
                    dve.wait_ge(first_in_slot[b % 2], 16 * BT * (b // 2))
                for t in range(BT):
                    last = nc.vector.tensor_scalar(first_row[b % 2][:, t, 0:D], x2[:, t, :], mean_var[:, t, 0:1],
                                                   rstd[:, t:t + 1], ALU.subtract, ALU.mult)
                    if t % 2:
                        last.then_inc(xn_ok, 1)

            def route(b):
                dve.wait_ge(logit_ps_ok, b + 1)
                then(nc.vector.tensor_scalar(logits[:], logit_ps, inv_temp[:, 0:1], None, ALU.mult))
                values = logits
                for k in range(TOP):
                    then(nc.vector.tensor_reduce(top[k][:], values[:], AX.X, ALU.max))
                    then(nc.vector.tensor_tensor(rank[:], values[:], wide(top[k][:]), ALU.is_equal))
                    then(nc.vector.tensor_tensor(rank[:], rank[:], order[:], ALU.mult))
                    then(nc.vector.tensor_reduce(key[:], rank[:], AX.X, ALU.max))
                    then(nc.vector.tensor_tensor(one_hot[k][:], order[:], wide(key[:]), ALU.is_equal))
                    if k == 0:
                        then(nc.vector.tensor_scalar(second[:], one_hot[0][:], -BIG, BIG / 2, ALU.mult,
                                                     ALU.add))
                        then(nc.vector.tensor_tensor(second[:], second[:], logits[:], ALU.min))
                        values = second
                nc.vector.tensor_tensor(chosen[:].rearrange("p e t -> p t e"), one_hot[0][:], one_hot[1][:],
                                        ALU.add).then_inc(chosen_ok, 1)
                nc.vector.tensor_tensor(gap[:], top[1][:], top[0][:], ALU.subtract).then_inc(gap_ok, 1)
                then(nc.vector.tensor_tensor(base[:], region[:], start[:], ALU.add))
                dve.wait_ge(power_ok, b + 1)
                then(nc.vector.tensor_scalar(total[:], power[:], 1.0, None, ALU.add))
                then(nc.vector.reciprocal(total[:], total[:]))
                nc.vector.tensor_copy(first_row[b % 2][:, :, ROW_W], total[:])
                nc.vector.tensor_copy(first_row[b % 2][:, :, ROW_ID].bitcast(I32), token_f[:])
                nc.vector.tensor_tensor(second_weight[b % 2][:], power[:], total[:], ALU.mult)
                nc.vector.tensor_copy(token_id[b % 2][:], token_f[:])
                then(nc.vector.tensor_scalar(token_f[:], token_f[:], float(SEQ), None, ALU.add))
                dve.wait_ge(counts_ok, b + 1)
                then(nc.vector.tensor_tensor_scan(running[:].rearrange("p e t -> p (e t)"), ones_row[:],
                                                  router_ps[:, 2, :], 0.0, ALU.mult, ALU.add))
                then(nc.vector.tensor_tensor(place[:], running[:], total_ps, ALU.subtract))
                then(nc.vector.tensor_tensor(count[:], running[:, :, BT - 1], place[:, :, 0], ALU.subtract))
                then(nc.vector.tensor_tensor(base[:], base[:], place[:, :, 0], ALU.subtract))
                then(nc.vector.tensor_tensor(place[:], place[:], wide(base[:], BT), ALU.add))
                then(nc.vector.tensor_tensor(place[:], place[:], prefix_ps, ALU.add))
                then(nc.vector.tensor_tensor(start[:], start[:], count[:], ALU.add))
                for k in range(TOP):
                    then(nc.vector.tensor_tensor(picked[:], one_hot[k][:], place[:].rearrange("p e t -> p t e"),
                                                 ALU.mult))
                    then(nc.vector.tensor_reduce(slot_f[:], picked[:], AX.X, ALU.add))
                    nc.vector.tensor_copy(slot[b % 2][:, k, :], slot_f[:]).then_inc(slot_ok, 1)

            def tables():
                then(nc.vector.tensor_tensor(pad_slot_f[:], region[:], start[:], ALU.add))
                nc.vector.tensor_copy(pad_slot[:], pad_slot_f[0:1, :]).then_inc(pad_slot_ok, 1)
                then(nc.vector.tensor_scalar(filled[:], start[:], 1.0 / P, None, ALU.mult))
                then(nc.vector.tensor_tensor(passed, filled[:].unsqueeze(1).to_broadcast(
                    [P, SLOT_TILES + 1, EXPERTS]), wide(tile_index[:]), ALU.is_gt))
                then(nc.vector.tensor_reduce(tiles[:], passed.rearrange("p n e -> p e n"), AX.X, ALU.add))
                then(nc.vector.tensor_tensor_scan(tiles_end[:], ones_row[:, 0:EXPERTS], tiles[:], 0.0, ALU.mult,
                                                  ALU.add))
                then(nc.vector.tensor_scalar(jump[:], tiles[:], -float(P), float(REGION), ALU.mult, ALU.add))
                then(nc.vector.tensor_tensor(passed, wide(tile_index[:]),
                                             tiles_end[:].unsqueeze(1).to_broadcast([P, SLOT_TILES + 1, EXPERTS]),
                                             ALU.is_ge))
                then(nc.vector.tensor_reduce(tile_f[:], passed, AX.X, ALU.add))
                then(nc.vector.tensor_scalar(tile_expert[:], tile_f[0:1, :], float(EXPERTS - 1), None, ALU.min))
                then(nc.vector.tensor_tensor(passed, passed,
                                             jump[:].unsqueeze(1).to_broadcast([P, SLOT_TILES + 1, EXPERTS]),
                                             ALU.mult))
                then(nc.vector.tensor_reduce(tile_f[:], passed, AX.X, ALU.add))
                then(nc.vector.scalar_tensor_tensor(out=tile_row[:], in0=tile_index[0:1, :], scalar=float(P),
                                                    in1=tile_f[0:1, :], op0=ALU.mult, op1=ALU.add))

            nc.vector.memset(ones[:], 1.0)
            nc.vector.memset(start[:], 0.0)
            then(nc.vector.memset(ones_row[:], 1.0))
            invert(0)
            normalise(0)
            residual(0)
            invert(1)
            statistics(0)
            dve.wait_ge(small_in, 48)
            then(nc.vector.reciprocal(inv_temp[:], temp_in[:]))
            dve.wait_ge(const_ok, 7)
            for b in range(BATCH):
                if b + 1 < BATCH:
                    normalise(b + 1)
                layer_norm(b)
                if b + 1 < BATCH:
                    residual(b + 1)
                    if b + 2 < BATCH:
                        invert(b + 2)
                    statistics(b + 1)
                route(b)
            tables()

        @block.scalar
        def _(act):
            def take_root(b):
                act.wait_ge(inv_var_ok, b + 1)
                nc.scalar.activation(root[:], inv_var[:], ACT.Sqrt).then_inc(root_ok, 1)

            take_root(0)
            for b in range(BATCH):
                for t in range(PAIRS):
                    act.wait_ge(xnT_ps_ok, b * PAIRS + t + 1)
                    nc.scalar.activation(xnT[t % 2][:].rearrange("p t c n -> p (t c n)"), xnT_ps[:],
                                         ACT.Copy).then_inc(xnT_ok, 1)
                if b + 1 < BATCH:
                    take_root(b + 1)
                act.wait_ge(gap_ok, b + 1)
                nc.scalar.activation(power[:], gap[:], ACT.Exp).then_inc(power_ok, 1)
                if b:
                    act.wait_ge(second_in_slot, 16 * BT * b)
                nc.scalar.activation(second_row[:, :, 0:D], first_row[b % 2][:, :, 0:D],
                                     ACT.Copy).then_inc(copy_ok, 1)

        @block.tensor
        def _(pe):
            def spread_out(b, k):
                n = b * SPREADS + k
                if k == 0:
                    pe.wait_ge(inv_den_ok, b + 1)
                if n >= 2:
                    pe.wait_ge(heads_ok, n - 1)
                for t in range(TPC):
                    last = nc.tensor.matmul(spread_ps[n % 2][:, t * P:(t + 1) * P],
                                            spread[:, k % DC, k // DC * TPC + t, :], inv_den[:], start=True, stop=True)
                last.then_inc(spread_ps_ok, 1)

            def project(b, t):
                n = b * PAIRS + t
                pe.wait_ge(heads_ok, b * SPREADS + (2 * t * P // CHUNK + 1) * DC)
                if b:
                    pe.wait_ge(x2_ok, n - PAIRS + 1)
                for i in range(2):
                    for c in range(DC):
                        last = nc.tensor.matmul(proj_ps[t][:, i, :], heads[:, c, (2 * t + i) * P:(2 * t + i + 1) * P],
                                                wo[:, c, :], start=(c == 0), stop=(c == DC - 1))
                last.then_inc(proj_ok, 1)

            def normal_turned(b, t):
                n = b * PAIRS + t
                pe.wait_ge(xn_ok, n + 1)
                if n >= 1:
                    pe.wait_ge(xnT_ok, n)
                for i in range(2):
                    for c in range(DC):
                        last = nc.tensor.transpose(xnT_ps[:, (i * DC + c) * P:(i * DC + c + 1) * P],
                                                   first_row[b % 2][:, 2 * t + i, c * P:(c + 1) * P], ident[:])
                last.then_inc(xnT_ps_ok, 1)

            def router(b, t):
                pe.wait_ge(xnT_ok, b * PAIRS + t + 1)
                if t == 0 and b:
                    pe.wait_ge(slot_ok, TOP * b)
                for i in range(2):
                    for c in range(DC):
                        last = nc.tensor.matmul(logit_ps[:, 2 * t + i, :], xnT[t % 2][:, i, c, :], wr[:, c, :],
                                                start=(c == 0), stop=(c == DC - 1))
                if t == PAIRS - 1:
                    last.then_inc(logit_ps_ok, 1)

            def counts(b):
                pe.wait_ge(chosen_ok, b + 1)
                flat = chosen[:].rearrange("p e t -> p (e t)")
                nc.tensor.matmul(router_ps[:, 1, :], before[:], flat, start=True, stop=True)
                nc.tensor.matmul(router_ps[:, 2, :], ones[:], flat, start=True,
                                 stop=True).then_inc(counts_ok, 1)

            pe.wait_ge(const_ok, 1)
            for k in range(SPREADS):
                spread_out(0, k)
            pe.wait_ge(const_ok, 3)
            pe.wait_ge(small_in, 48)
            for t in range(PAIRS):
                project(0, t)
            for b in range(BATCH):
                if b + 1 < BATCH:
                    for k in range(SPREADS):
                        spread_out(b + 1, k)
                    for t in range(PAIRS):
                        project(b + 1, t)
                for t in range(PAIRS + 1):
                    if t < PAIRS:
                        normal_turned(b, t)
                    if t:
                        router(b, t - 1)
                counts(b)


def expert_phase(nc, dram, weights, ident, tile_expert, tile_row, out):
    with ExitStack() as ctx:
        def sb(name, shape, dt=F32):
            return ctx.enter_context(nc.sbuf_tensor(name, shape, dt))

        def ps(name, shape, dt=F32):
            return ctx.enter_context(nc.psum_tensor(name, shape, dt))

        def sem(name):
            return ctx.enter_context(nc.semaphore(name))

        U, B = SLOT_UNROLL, ROW_BUFS
        LOOPS = (SLOT_TILES - SLOT_LEAD) // U
        w1_sb, w2_sb, bias, loaded = weights
        rows = [sb(f"e_rows{n}", [P, ROW]) for n in range(B)]
        rowsT = [sb(f"e_rowsT{n}", [P, D]) for n in range(2)]
        g_sum = [sb(f"e_g_sum{n}", [P, FF]) for n in range(2)]
        gate = [sb(f"e_gate{n}", [P, FF]) for n in range(2)]
        hidden = [sb(f"e_hidden{n}", [P, FF]) for n in range(2)]
        hiddenT = [sb(f"e_hiddenT{n}", [P, FF]) for n in range(2)]
        token = [sb(f"e_token{n}", [P, 1], I32) for n in range(B)]
        y = [sb(f"e_y{n}", [P, D]) for n in range(B)]

        rowsT_ps = ps("e_rowsT_ps", [P, D])
        a_ps = [ps(f"e_a_ps{n}", [P, FF]) for n in range(2)]
        g_ps = [ps(f"e_g_ps{n}", [P, FF]) for n in range(2)]
        hiddenT_ps = ps("e_hiddenT_ps", [P, FF])
        y_ps = [ps(f"e_y_ps{n}", [P, D]) for n in range(2)]

        rows_ok = [sem(f"e_rows_ok{n}") for n in range(B)]
        rowsT_ps_ok = sem("e_rowsT_ps_ok")
        rowsT_ok = sem("e_rowsT_ok")
        g_ok = sem("e_g_ok")
        a_ok = sem("e_a_ok")
        g_sum_ok = sem("e_g_sum_ok")
        a_sum_ok = sem("e_a_sum_ok")
        y_sum_ok = sem("e_y_sum_ok")
        gate_ok = sem("e_gate_ok")
        hidden_ok = sem("e_hidden_ok")
        hiddenT_ps_ok = sem("e_hiddenT_ps_ok")
        hiddenT_ok = sem("e_hiddenT_ok")
        y_ps_ok = sem("e_y_ps_ok")
        token_ok = sem("e_token_ok")
        y_ok = sem("e_y_ok")
        turn = sem("e_turn")
        added = sem("e_added")
        landed = sem("e_landed")
        block = ctx.enter_context(nc.Block())

        def steps(eng, step):
            for n in range(SLOT_LEAD):
                step(n, n, n)
            with eng.Fori(0, LOOPS) as it:
                for t in range(SLOT_LEAD, SLOT_LEAD + U):
                    step(it * U + t, t, None)
            for n in range(SLOT_TILES, SLOT_TILES + 2):
                step(n, n, n)

        def cycle(n, c, back=0):
            if isinstance(n, int):
                return (n - back) // B
            return (n - c) // B + (c - back) // B

        @block.sync
        def _(sp):
            def load(n, c):
                row = sp.value_load(tile_row[0:1, n:n + 1] if isinstance(n, int) else tile_row[0:1, bass.ds(n, 1)],
                                    min_val=0, max_val=EXPERTS * REGION + (SPARE - 1) * P)
                sp.dma_start(rows[c % B][:], dram["rows"][bass.ds(row, P), :]).then_inc(rows_ok[c % B], 16)

            for n in range(SLOT_LEAD + 1):
                if n >= B:
                    sp.wait_ge(y_ok, n + 1)
                load(n, n)
            with sp.Fori(0, LOOPS) as it:
                for c in range(SLOT_LEAD, SLOT_LEAD + U):
                    sp.wait_ge(y_ok, it * U + c + 2)
                    load(it * U + c + 1, c + 1)

        @block.gpsimd
        def _(pool):
            pool.sem_inc(landed, B)

            def add(n, c):
                pool.wait_ge(y_ok, n + 1 + B)
                pool.sem_inc(turn, 1)
                nc.gpsimd.indirect_dma_start(
                    out=out, out_offset=bass.IndirectOffsetOnAxis(ap=token[c % B][:], axis=0), in_=y[c % B][:],
                    in_offset=None, compute_op=ALU.add).then_inc(added, 16)
                pool.wait_ge(added, (n + 1) * 16)
                pool.sem_inc(landed, 1)

            for n in range(SLOT_LEAD):
                add(n, n)
            with pool.Fori(0, LOOPS) as it:
                for c in range(SLOT_LEAD, SLOT_LEAD + U):
                    add(it * U + c, c)

        @block.vector
        def _(dve):
            dve.sem_inc(y_ok, B)
            dve.wait_ge(loaded, 16 * (3 * EXPERTS + FC))

            def rows_turned(n, c):
                dve.wait_ge(rowsT_ps_ok, n + 1)
                nc.vector.tensor_copy(rowsT[c % 2][:], rowsT_ps[:]).then_inc(rowsT_ok, 1)

            def expert_of(n):
                return dve.value_load(tile_expert[0:1, n:n + 1] if isinstance(n, int) else
                                      tile_expert[0:1, bass.ds(n, 1)], min_val=0, max_val=EXPERTS - 1)

            def bias_of(expert, layer, first, width):
                return bias[layer][:, bass.ds(expert, 1), first:first + width].rearrange("p e n -> p (e n)")

            def gated(n, c):
                expert = expert_of(n)
                dve.wait_ge(g_ok, n + 1)
                nc.vector.tensor_tensor(g_sum[c % 2][:], g_ps[c % 2][:], bias_of(expert, 0, FF, FF),
                                        ALU.add).then_inc(g_sum_ok, 1)
                dve.wait_ge(a_ok, n + 1)
                nc.vector.tensor_tensor(hidden[c % 2][:], a_ps[c % 2][:], bias_of(expert, 0, 0, FF),
                                        ALU.add).then_inc(a_sum_ok, 1)
                dve.wait_ge(a_sum_ok, n + 1)
                dve.wait_ge(gate_ok, n + 1)
                nc.vector.tensor_tensor(hidden[c % 2][:], hidden[c % 2][:], gate[c % 2][:],
                                        ALU.mult).then_inc(hidden_ok, 1)

            def weighted(n, c):
                expert = expert_of(n)
                dve.wait_ge(landed, n + 1)
                dve.wait_ge(y_ps_ok, n + 1)
                nc.vector.tensor_tensor(y[c % B][:], y_ps[c % 2][:], bias_of(expert, 1, 0, D),
                                        ALU.add).then_inc(y_sum_ok, 1)
                nc.vector.tensor_copy(token[c % B][:], rows[c % B][:, ROW_ID:ROW].bitcast(I32)).then_inc(token_ok, 1)
                dve.wait_ge(y_sum_ok, n + 1)
                nc.vector.tensor_scalar(y[c % B][:], y[c % B][:], rows[c % B][:, ROW_W:ROW_W + 1], None,
                                        ALU.mult).then_inc(y_ok, 1)

            def step(n, c, value):
                if value is None or n + 1 < SLOT_TILES:
                    rows_turned(n + 1, c + 1)
                if value is None or n < SLOT_TILES:
                    gated(n, c)
                if value is None or n >= 2:
                    weighted(n - 2, c - 2)

            rows_turned(0, 0)
            steps(dve, step)

        @block.scalar
        def _(act):
            def silu(n, c):
                act.wait_ge(g_sum_ok, n + 1)
                nc.scalar.activation(gate[c % 2][:], g_sum[c % 2][:], ACT.Silu).then_inc(gate_ok, 1)

            def hidden_turned(n, c):
                act.wait_ge(hiddenT_ps_ok, n + 1)
                nc.scalar.activation(hiddenT[c % 2][:], hiddenT_ps[:], ACT.Copy).then_inc(hiddenT_ok, 1)

            def step(n, c, value):
                if value is None or n < SLOT_TILES:
                    silu(n, c)
                if value is None or 1 <= n <= SLOT_TILES:
                    hidden_turned(n - 1, c - 1)

            steps(act, step)

        @block.tensor
        def _(pe):
            def rows_turned(n, c):
                pe.wait_ge(rows_ok[c % B], (cycle(n, c) + 1) * 16)
                if not isinstance(n, int) or n >= 1:
                    pe.wait_ge(rowsT_ok, n)
                for d in range(DC):
                    last = nc.tensor.transpose(rowsT_ps[:, d * P:(d + 1) * P], rows[c % B][:, d * P:(d + 1) * P],
                                               ident[:])
                last.then_inc(rowsT_ps_ok, 1)

            def expert_of(n):
                return pe.value_load(tile_expert[0:1, n:n + 1] if isinstance(n, int) else
                                     tile_expert[0:1, bass.ds(n, 1)], min_val=0, max_val=EXPERTS - 1)

            def up(n, c, expert):
                pe.wait_ge(rowsT_ok, n + 1)
                for out_ps, first, done in ((g_ps[c % 2], FF, g_ok), (a_ps[c % 2], 0, a_ok)):
                    for d in range(DC):
                        last = nc.tensor.matmul(out_ps[:], rowsT[c % 2][:, d * P:(d + 1) * P],
                                                w1_sb[:, bass.ds(expert, 1), d, first:first + FF].rearrange(
                                                    "p e n -> p (e n)"), start=(d == 0), stop=(d == DC - 1))
                    last.then_inc(done, 1)

            def hidden_turned(n, c):
                pe.wait_ge(hidden_ok, n + 1)
                for f in range(FC):
                    last = nc.tensor.transpose(hiddenT_ps[:, f * P:(f + 1) * P], hidden[c % 2][:, f * P:(f + 1) * P],
                                               ident[:])
                last.then_inc(hiddenT_ps_ok, 1)

            def down(n, c, expert):
                pe.wait_ge(y_ok, n - 1 + B)
                pe.wait_ge(hiddenT_ok, n + 1)
                for f in range(FC):
                    last = nc.tensor.matmul(y_ps[c % 2][:], hiddenT[c % 2][:, f * P:(f + 1) * P],
                                            w2_sb[f][:, bass.ds(expert, 1), :].rearrange("p e n -> p (e n)"),
                                            start=(f == 0), stop=(f == FC - 1))
                last.then_inc(y_ps_ok, 1)

            def step(n, c, value):
                if value is None or n + 1 < SLOT_TILES:
                    rows_turned(n + 1, c + 1)
                if value is None or n < SLOT_TILES:
                    up(n, c, expert_of(n))
                if value is None or n >= 2:
                    down(n - 2, c - 2, expert_of(n - 2))
                if value is None or 1 <= n <= SLOT_TILES:
                    hidden_turned(n - 1, c - 1)

            rows_turned(0, 0)
            pe.wait_ge(loaded, 16 * (3 * EXPERTS + FC))
            steps(pe, step)


def build(nc, x, w_dkv, w_uk, w_uv, w_uq, w_o, w_r, temp, w1, b1, w2, b2, out):
    dram = {
        "q_parts": nc.dram_tensor("q_parts", [DC, PARTS, P, NTOK], BF16).ap(),
        "k_parts": nc.dram_tensor("k_parts", [DC, PARTS, P, NTOK], BF16).ap(),
        "v": nc.dram_tensor("v_rows", [NTOK, D], F32).ap(),
        "ctx": nc.dram_tensor("ctx_cols", [NQUAD, P, SEQ], F32).ap(),
        "den": nc.dram_tensor("ctx_dens", [BATCH * HEADS, SEQ], F32).ap(),
        "rows": nc.dram_tensor("slot_rows", [EXPERTS * REGION + SPARE * P, ROW], F32).ap(),
    }
    x = x.rearrange("b t d -> (b t) d")
    project_phase(nc, dram, x, w_dkv, w_uk, w_uv, w_uq)
    with ExitStack() as ctx:
        w1_sb = ctx.enter_context(nc.sbuf_tensor("w1_sb", [P, EXPERTS, DC, 2 * FF], F32))
        w2_early = [ctx.enter_context(nc.sbuf_tensor(f"w2_sb{f}", [P, EXPERTS, D], F32)) for f in range(FC_EARLY)]
        loaded = ctx.enter_context(nc.semaphore("loaded"))
        attention_phase(nc, dram, w1, w1_sb, w2, w2_early, loaded)
        mixed_phase(nc, dram, x, w_o, w_r, temp, (b1, b2), w2, w1_sb, w2_early, loaded, out)


_INS = ["L0_attn_x", "L0_attn_W_DKV", "L0_attn_W_UK", "L0_attn_W_UV", "L0_attn_W_UQ", "L0_attn_W_O", "L0_ffn_Wr",
        "L0_ffn_temp", "L0_ffn_W1", "L0_ffn_b1", "L0_ffn_W2", "L0_ffn_b2"]


def kernel(**inputs):
    import numpy as _np
    import concourse.bacc as _bacc
    from concourse.bass_utils import run_bass_kernel_spmd as _run

    nc = _bacc.Bacc("TRN2", target_bir_lowering=False, num_devices=1)
    arrays, args = {}, []
    for name in _INS:
        a = _np.ascontiguousarray(inputs[name])
        arrays[f"in_{name}"] = a
        args.append(nc.dram_tensor(f"in_{name}", a.shape, mybir.dt.from_np(a.dtype), kind="ExternalInput").ap())
    args.append(nc.dram_tensor("out_dram", (OUT_ROWS, D), F32, kind="ExternalOutput").ap())
    build(nc, *args)
    r = _run(nc, [arrays], core_ids=[0])
    return r.results[0]["out_dram"][:NTOK].reshape(BATCH, SEQ, D)
```
